# Optimizing a Trainium2 kernel written in Bass

```python
import numpy as np
import jax
import jax.numpy as jnp

def _softmax(x, axis=-1):
    return jax.nn.softmax(x, axis=axis)

def _gelu(x):
    return jax.nn.gelu(x, approximate=True)

def _silu(x):
    return jax.nn.silu(x)

def _sigmoid(x):
    return jax.nn.sigmoid(x)

def _layernorm(x, axis=-1, eps=1e-05):
    m = jnp.mean(x, axis=axis, keepdims=True)
    v = jnp.var(x, axis=axis, keepdims=True)
    return (x - m) / jnp.sqrt(v + eps)

def _scatter_add(tgt, idx, src, axis=0):
    return tgt.at[idx].add(src)

def _segment_sum(src, seg, n):
    return jax.ops.segment_sum(src, seg, n)
kernel_name = 'mk_seq_preln_d1_jaxref_r8_99ad74'

def setup_inputs(seed: int=0):
    np.random.seed(seed)
    _w = jnp.asarray

    def _L0_attn_setup():
        import jax, jax.numpy as jnp
        import numpy as np
        import math
        HIDDEN = 512
        NUM_HEADS = 32
        HEAD_DIM = HIDDEN // NUM_HEADS
        SCALE = 1.0 / HEAD_DIM

        def _alibi_slopes(n_heads: int) -> np.ndarray:
            cp2 = 2 ** math.floor(math.log2(n_heads))
            base = 2 ** (-2 ** (-(math.log2(cp2) - 3)))
            slopes = base ** np.arange(1, cp2 + 1, dtype=np.float32)
            if cp2 != n_heads:
                extra_base = 2 ** (-2 ** (-(math.log2(2 * cp2) - 3)))
                n_rem = min(cp2, n_heads - cp2)
                extra = extra_base ** np.arange(1, 1 + 2 * n_rem, 2, dtype=np.float32)
                slopes = np.concatenate([slopes, extra])
            return slopes.astype(np.float32)
        key = jax.random.key(seed)
        k1, k2, k3, k4, k5 = jax.random.split(key, 5)
        B, S = (2, 256)
        return {'hidden_states': jax.random.normal(k1, (B, S, HIDDEN), dtype=jnp.float32), 'w_attn': jax.random.normal(k2, (HIDDEN, 3 * HIDDEN), dtype=jnp.float32) * 0.02, 'b_attn': jnp.zeros((3 * HIDDEN,), dtype=jnp.float32), 'w_proj': jax.random.normal(k3, (HIDDEN, HIDDEN), dtype=jnp.float32) * 0.02, 'b_proj': jnp.zeros((HIDDEN,), dtype=jnp.float32)}
    _L0_attn_in = _L0_attn_setup()

    def _L0_ffn_setup():
        import jax, jax.numpy as jnp
        import numpy as np
        HIDDEN = 512
        INTER = 1376
        key = jax.random.key(seed)
        k0, k1, k2, k3 = jax.random.split(key, 4)
        scale_h = 1.0 / np.sqrt(HIDDEN)
        scale_i = 1.0 / np.sqrt(INTER)
        return {'x': jax.random.normal(k0, (4, 32, HIDDEN), dtype=jnp.float32), 'w_gate': jax.random.normal(k1, (INTER, HIDDEN), dtype=jnp.float32) * scale_h, 'w_up': jax.random.normal(k2, (INTER, HIDDEN), dtype=jnp.float32) * scale_h, 'w_down': jax.random.normal(k3, (HIDDEN, INTER), dtype=jnp.float32) * scale_i}
    _L0_ffn_in = _L0_ffn_setup()
    _d = {'L0_attn_hidden_states': _L0_attn_in['hidden_states'], 'L0_attn_w_attn': _L0_attn_in['w_attn'], 'L0_attn_b_attn': _L0_attn_in['b_attn'], 'L0_attn_w_proj': _L0_attn_in['w_proj'], 'L0_attn_b_proj': _L0_attn_in['b_proj'], 'L0_ffn_w_gate': _L0_ffn_in['w_gate'], 'L0_ffn_w_up': _L0_ffn_in['w_up'], 'L0_ffn_w_down': _L0_ffn_in['w_down']}
    _x0 = _d['L0_attn_hidden_states']
    _d['L0_attn_hidden_states'] = jax.random.normal(jax.random.fold_in(jax.random.key(seed), 1), (4, 512, 512), dtype=_x0.dtype)
    del _x0
    return _d

def reference(L0_attn_hidden_states, L0_attn_w_attn, L0_attn_b_attn, L0_attn_w_proj, L0_attn_b_proj, L0_ffn_w_gate, L0_ffn_w_up, L0_ffn_w_down):

    def _L0_attn_ref(hidden_states, w_attn, b_attn, w_proj, b_proj):
        import jax, jax.numpy as jnp
        import numpy as np
        import math
        HIDDEN = 512
        NUM_HEADS = 32
        HEAD_DIM = HIDDEN // NUM_HEADS
        SCALE = 1.0 / HEAD_DIM

        def _alibi_slopes(n_heads: int) -> np.ndarray:
            cp2 = 2 ** math.floor(math.log2(n_heads))
            base = 2 ** (-2 ** (-(math.log2(cp2) - 3)))
            slopes = base ** np.arange(1, cp2 + 1, dtype=np.float32)
            if cp2 != n_heads:
                extra_base = 2 ** (-2 ** (-(math.log2(2 * cp2) - 3)))
                n_rem = min(cp2, n_heads - cp2)
                extra = extra_base ** np.arange(1, 1 + 2 * n_rem, 2, dtype=np.float32)
                slopes = np.concatenate([slopes, extra])
            return slopes.astype(np.float32)
        B, S, _ = hidden_states.shape
        H, D = (NUM_HEADS, HEAD_DIM)
        qkv = hidden_states @ w_attn + b_attn
        q, k, v = jnp.split(qkv, 3, axis=-1)
        q = q.reshape(B, S, H, D)
        k = k.reshape(B, S, H, D)
        v = v.reshape(B, S, H, D)
        scores = jnp.einsum('bqhd,bkhd->bhqk', q, k) * SCALE
        slopes = jnp.asarray(_alibi_slopes(H))
        pos = jnp.arange(S)
        rel = pos[None, :] - pos[:, None]
        bias = slopes[:, None, None] * rel[None, :, :]
        causal = rel <= 0
        scores = jnp.where(causal[None, None], scores + bias[None], -jnp.inf)
        attn = jax.nn.softmax(scores, axis=-1)
        out = jnp.einsum('bhqk,bkhd->bqhd', attn, v).reshape(B, S, HIDDEN)
        return out @ w_proj + b_proj

    def _L0_ffn_ref(x, w_gate, w_up, w_down):
        import jax, jax.numpy as jnp
        import numpy as np
        HIDDEN = 512
        INTER = 1376
        gate = jax.nn.silu(jnp.einsum('bsh,ih->bsi', x, w_gate))
        up = jnp.einsum('bsh,ih->bsi', x, w_up)
        return jnp.einsum('bsi,hi->bsh', gate * up, w_down)
    x = L0_attn_hidden_states
    x = x + _L0_attn_ref(_layernorm(x, axis=-1), L0_attn_w_attn, L0_attn_b_attn, L0_attn_w_proj, L0_attn_b_proj)
    x = x + _L0_ffn_ref(_layernorm(x, axis=-1), L0_ffn_w_gate, L0_ffn_w_up, L0_ffn_w_down)
    return x

_drawn_inputs = setup_inputs


def setup_inputs(seed=0):
    import zlib

    import numpy as np

    out = dict(_drawn_inputs(seed))
    spreads = {'L0_attn_b_attn': (0.0, 0.1), 'L0_attn_b_proj': (0.0, 0.1)}
    factors = {}
    for name, (base, spread) in spreads.items():
        noise = np.random.default_rng([zlib.crc32(name.encode()), seed]).standard_normal(out[name].shape)
        drawn = base * np.exp(spread * noise) if base else spread * noise
        out[name] = jnp.asarray(drawn.astype(out[name].dtype))
    for name, factor in factors.items():
        out[name] = (out[name] * factor).astype(out[name].dtype)
    return out
```

```python
from contextlib import ExitStack

import numpy as np

import concourse.bass as bass
from concourse import mybir

F32 = mybir.dt.float32
F32R = mybir.dt.float32r
BF16 = mybir.dt.bfloat16
ACT = mybir.ActivationFunctionType
ALU = mybir.AluOpType
AX = mybir.AxisListType

P = 128
B, S, D = 4, 512, 512
H, HD = 32, 16
F = 1376
KT = D // P
TT = S // P
HG = P // HD
G = H // HG
QUADS = HG // 4
FT = (F + P - 1) // P
EPS = 1e-5
NEG = -1e30

Q_TERM = (0, 1, 2, 0, 1, 0)
K_TERM = (0, 0, 0, 1, 1, 2)
TERMS = len(Q_TERM)
ROW_X = TERMS * HD
K_MAX = ROW_X + 1
K_EXP = ROW_X + 5

WIDE = (512, 512, 256)
COL0 = (0, 512, 1024)
NBLK = sum(WIDE) // P
PT_RING = 6

TILES = ([("T", k) for k in range(KT)] + [("Q", 0), ("K", 0), ("Q", 1), ("K", 1)]
         + [("V", t) for t in range(TT)] + [("M", 0), ("Q", 2), ("K", 2), ("M", 1)]
         + [("Q", 3), ("K", 3), ("M", 2), ("M", 3)] + [("P", t) for t in range(TT)])
NT = len(TILES)
TILE_AT = {t: n for n, t in enumerate(TILES)}
DENSE_BANKS = (7, 3, 4, 5)
BY_ACT = "TQKV"
BY_DVE = "TQKMP"


def act_reads(n):
    return sum(kind in BY_ACT for kind, _ in TILES[:n + 1])


def dve_reads(n):
    return sum(kind in BY_DVE for kind, _ in TILES[:n + 1])


ACT_READS, DVE_READS = act_reads(NT - 1), dve_reads(NT - 1)
STEPS = 1 + 2 * G + 2 * G * QUADS + 3


def slopes():
    start = 2.0 ** (-(2.0 ** -(np.log2(H) - 3)))
    return (start ** np.arange(1, H + 1, dtype=np.float32)).astype(np.float32)


def bf16_part(x):
    return (x.view(np.uint32) & np.uint32(0xFFFF0000)).view(np.float32)


def extra_rows():
    s, parts = slopes() * np.float32(HD), []
    for _ in range(3):
        p = bf16_part(s)
        parts.append(np.repeat(p[:, None], S, 1))
        s = s - p
    pos = np.arange(S, dtype=np.float32) - S // 2
    one = np.ones(S, np.float32)
    return np.concatenate(parts), np.stack([pos, one, pos, one, pos])


def rounds(b, per, k=0):
    return (b + 1) * per + k


def wait_apart(eng, apart, semaphore, value):
    eng.wait_ge(semaphore, value)
    eng.sem_inc(apart, 1)


def layernorm(dve, step, src, dst, stats, mv, rstd, moments_ready, rstd_ready, count):
    for t in range(TT):
        last = dve.bn_stats(stats[:, t, :], src[:, t, :])
    step(last)
    for t in range(TT):
        last = dve.bn_aggr(mv[:, t, :], stats[:, t, :])
    last.then_inc(moments_ready, 1)
    dve.wait_ge(moments_ready, count)
    dve.wait_ge(rstd_ready, count)
    for t in range(TT):
        last = dve.tensor_scalar(dst[:, t, :], src[:, t, :], mv[:, t, 0:1], rstd[:, t:t + 1], ALU.subtract, ALU.mult)
    return last


def inverse_deviation(pool, apart, mv, rstd, minus_half, moments_ready, var_ready, rstd_ready, count):
    wait_apart(pool, apart, moments_ready, count)
    pool.tensor_scalar(mv[:, :, 1], mv[:, :, 1], EPS, None, ALU.add).then_inc(var_ready, 1)
    pool.wait_ge(var_ready, count)
    pool.tensor_tensor(rstd[:, :], mv[:, :, 1], minus_half[:, :], ALU.pow).then_inc(rstd_ready, 1)


def kernel_body(nc, x_d, wqkv_d, bqkv_d, wproj_d, bproj_d, wgu_d, wd_d, qx_d, kx_d, out_d):
    with ExitStack() as whole:
        bank = [whole.enter_context(nc.psum_tensor(f"bank{i}", [P, 512], F32)) for i in range(8)]
        ident = whole.enter_context(nc.sbuf_tensor("ident", [P, P], F32))
        minus_half = whole.enter_context(nc.sbuf_tensor("minus_half", [P, TT], F32))
        x1_dram = nc.dram_tensor("x1_dram", [B, TT, P, D], F32, kind="Internal").ap()
        attention(nc, x_d, wqkv_d, bqkv_d, wproj_d, bproj_d, qx_d, kx_d, x1_dram, bank, ident, minus_half)
        ffn(nc, x1_dram, wgu_d, wd_d, out_d, bank, ident, minus_half)


def attention(nc, x_d, wqkv_d, bqkv_d, wproj_d, bproj_d, qx_d, kx_d, x1_dram, bank, ident, minus_half):
    x_v = x_d.rearrange("b (t p) d -> b t p d", p=P)
    parts_dram = nc.dram_tensor("parts_dram", [2, G, 3, P, S], BF16, kind="Internal").ap()
    slopes_dram = nc.dram_tensor("slopes_dram", [3, H, S], BF16, kind="Internal").ap()

    with ExitStack() as ctx:
        def sb(name, shape, dt=F32):
            return ctx.enter_context(nc.sbuf_tensor(name, shape, dt))

        def sem(name):
            return ctx.enter_context(nc.semaphore(name))

        wqkv_hi = sb("wqkv_hi", [P, KT, 3 * D], F32R)
        wqkv_lo = sb("wqkv_lo", [P, KT, 3 * D], F32R)
        wproj_hi = sb("wproj_hi", [P, KT, D], F32R)
        wproj_lo = sb("wproj_lo", [P, KT, D], F32R)
        bias_qkv = sb("bias_qkv", [P, 3 * G])
        bproj = sb("bproj", [P, D])
        identb = sb("identb", [P, P], BF16)
        mask_qk = sb("mask_qk", [P, P], BF16)
        mask_kq = sb("mask_kq", [P, P], BF16)
        xt = sb("xt", [P, TT, D])
        stats = sb("stats", [P, TT, 6])
        mv = sb("mv", [P, TT, 2])
        rstd = sb("rstd", [P, TT])
        fT_hi = sb("fT_hi", [P, KT, S], F32R)
        fT_lo = sb("fT_lo", [P, KT, S], F32R)
        part = sb("part", [P, 2, 3, S], BF16)
        rest = sb("rest", [P, 2, S])
        q_st = sb("q_st", [P, 2, HG, S], BF16)
        k_st = sb("k_st", [P, 2, HG, S], BF16)
        pt = sb("pt", [P, PT_RING, NBLK * P])
        v_nat = sb("v_nat", [P, TT, H, 2 * HD])
        bm = sb("bm", [P, HG, NBLK])
        mx = sb("mx", [P, HG, TT])
        mparts = sb("mparts", [P, 2, HG * TT], BF16)
        mt = sb("mt", [2 * HG * TT, P], BF16)
        rden = sb("rden", [P, S])
        on = sb("on", [P, QUADS, S])
        attnT = sb("attnT", [P, G, S])
        xr = sb("xr", [P, 2, D])
        qx_sb = sb("qx_sb", [3 * H, S], BF16)
        wqkv_raw = pt[:, :, :].rearrange("p a b -> p (a b)")[:, 0:KT * 3 * D].rearrange("p (k n) -> p k n", k=KT)
        wproj_raw = v_nat[:, :, :, :].rearrange("p t h e -> p (t h e)")[:, 0:KT * D].rearrange("p (k n) -> p k n", k=KT)
        qx_raw = attnT[0:3 * H, 0, :]
        kx_raw = on[ROW_X:K_EXP, 0, :]

        consts_in = sem("consts_in")
        wqkv_in = sem("wqkv_in")
        wproj_in = sem("wproj_in")
        zeroed = sem("zeroed")
        masks_made = sem("masks_made")
        w_hi_done = sem("w_hi_done")
        w_split = sem("w_split")
        w_split_v = sem("w_split_v")
        setup_done = sem("setup_done")
        slopes_cast = sem("slopes_cast")
        slopes_stored = sem("slopes_stored")
        x_in = [sem(f"x_in{t}") for t in range(TT)]
        step_done = sem("step_done")
        apart = {e: sem(f"apart_{e}") for e in ("sp", "pool", "dve", "pe")}
        moments_ready = sem("moments_ready")
        var_ready = sem("var_ready")
        rstd_ready = sem("rstd_ready")
        normed = sem("normed")
        tile_done = sem("tile_done")
        act_read = sem("act_read")
        dve_read = sem("dve_read")
        p2_done = sem("p2_done")
        p3_done = sem("p3_done")
        parts_stored = [sem("q_stored"), sem("k_stored")]
        stacked = [sem(f"stacked{s}") for s in range(2)]
        s_done = sem("s_done")
        s_maxed = sem("s_maxed")
        m_ready = sem("m_ready")
        m_placed = sem("m_placed")
        t_done = sem("t_done")
        exp_done = sem("exp_done")
        pv_done = sem("pv_done")
        pv_read = sem("pv_read")
        on_moved = [sem(f"on_moved{q}") for q in range(QUADS)]
        attn_hi = sem("attn_hi")
        attn_split = sem("attn_split")
        xr_in = [sem(f"xr_in{s}") for s in range(2)]
        x1_ready = sem("x1_ready")
        x1_stored = [sem(f"x1_stored{s}") for s in range(2)]
        block = ctx.enter_context(nc.Block())

        UNITS = 3 * H
        HU = 3 * HG
        NQ = G * QUADS
        STACK_DMAS = 2 * TERMS + 1

        @block.sync
        def _(sp):
            sp.dma_start(wqkv_raw, wqkv_d.rearrange("(k p) n -> p k n", p=P)).then_inc(wqkv_in, 16)
            sp.dma_start(wproj_raw, wproj_d.rearrange("(k p) n -> p k n", p=P)).then_inc(wproj_in, 16)
            sp.dma_start(qx_raw, qx_d).then_inc(consts_in, 16)
            sp.dma_start(kx_raw, kx_d).then_inc(consts_in, 16)
            with nc.allow_non_contiguous_dma(reason="biases, once, a column per partition"):
                sp.dma_start(bias_qkv[:, :], bqkv_d.rearrange("(c p) -> p c", p=P)).then_inc(consts_in, 16)
            sp.dma_start(bproj[:, :], bproj_d.rearrange("(a d) -> a d", a=1).broadcast_to([P, D])).then_inc(consts_in, 16)
            for s, n in ([(x, 16) for x in x_in] + [(x, G * 16) for x in parts_stored] + [(m_placed, G * 32)]
                         + [(x, G // 2 * STACK_DMAS * 16) for x in stacked] + [(x, G * 64) for x in on_moved]
                         + [(x, TT // 2 * 16) for x in xr_in + x1_stored]):
                sp.sem_inc(s, n)
            sp.wait_ge(slopes_cast, 1)
            sp.dma_start(slopes_dram.rearrange("a h s -> (a h) s"), qx_sb[:, :]).then_inc(slopes_stored, 16)
            sp.wait_ge(slopes_stored, 16)
            sp.wait_ge(setup_done, 1)
            with sp.Fori(0, B) as b:
                wait_apart(sp, apart["sp"], tile_done, rounds(b - 1, NT, KT))
                for t in range(TT):
                    sp.dma_start(xt[:, t, :], x_v[b, t]).then_inc(x_in[t], 16)

                def store_parts(g):
                    for c in range(2):
                        sp.wait_ge(p3_done, rounds(b, 2 * G, 2 * g + c + 1))
                        sp.dma_start(parts_dram[c, g].rearrange("a p s -> p a s"), part[:, c, :, :]).then_inc(parts_stored[c], 16)

                def load_stacks(g):
                    s = g % 2
                    wait_apart(sp, apart["sp"], t_done, rounds(b, UNITS, HU * (g - 1)))
                    for c, st, term in ((0, q_st, Q_TERM), (1, k_st, K_TERM)):
                        sp.wait_ge(parts_stored[c], rounds(b, G * 16, (g + 1) * 16))
                        for r in range(TERMS):
                            sp.dma_start(st[r * HD:(r + 1) * HD, s, :, :],
                                         parts_dram[c, g, term[r]].rearrange("(h e) s -> e h s", e=HD)).then_inc(stacked[s], 16)
                    sp.dma_start(q_st[ROW_X:K_EXP:2, s, :, :], slopes_dram[:, g * HG:(g + 1) * HG, :]).then_inc(stacked[s], 16)

                def place_maxima(g):
                    n = HG * TT
                    sp.wait_ge(dve_read, rounds(b, DVE_READS, dve_reads(TILE_AT["M", g])))
                    for a in range(2):
                        row = ROW_X + 1 + 2 * a
                        sp.dma_start(q_st[row:row + 1, g % 2, :, :].rearrange("p h (t n) -> p (h t) n", n=P),
                                     mt[a * n:(a + 1) * n, :]).then_inc(m_placed, 16)

                def compact(g):
                    sp.wait_ge(attn_split, rounds(b - 1, G, g + 1))
                    for q in range(QUADS):
                        sp.wait_ge(pv_read, rounds(b, NQ, g * QUADS + q + 1))
                        for j in range(4):
                            at = (q * 4 + j) * HD
                            sp.dma_start(attnT[at:at + HD, g, :], on[32 * j:32 * j + HD, q, :]).then_inc(on_moved[q], 16)

                store_parts(0)
                load_stacks(0)
                store_parts(1)
                load_stacks(1)
                place_maxima(0)
                compact(0)
                place_maxima(1)
                store_parts(2)
                load_stacks(2)
                compact(1)
                place_maxima(2)
                store_parts(3)
                load_stacks(3)
                compact(2)
                place_maxima(3)
                for t in range(2):
                    wait_apart(sp, apart["sp"], x1_stored[t], rounds(b - 1, 32, 32))
                    sp.dma_start(xr[:, t, :], x_v[b, t]).then_inc(xr_in[t], 16)
                compact(3)
                for t in range(TT):
                    wait_apart(sp, apart["sp"], x1_ready, rounds(b, TT, t + 1))
                    sp.dma_start(x1_dram[b, t], xr[:, t % 2, :]).then_inc(x1_stored[t % 2], 16)
                    if t < 2:
                        wait_apart(sp, apart["sp"], x1_stored[t], rounds(b, 32, 16))
                        sp.dma_start(xr[:, t, :], x_v[b, t + 2]).then_inc(xr_in[t], 16)
            for t in range(2):
                sp.wait_ge(x1_stored[t], rounds(B - 1, 32, 32))

        @block.gpsimd
        def _(pool):
            for m in (ident, identb, mask_qk, mask_kq):
                pool.memset(m[:, :], 0.0).then_inc(zeroed, 1)
            pool.memset(minus_half[:, :], -0.5).then_inc(zeroed, 1)
            pool.wait_ge(zeroed, 5)
            for m in (ident, identb):
                pool.affine_select(out=m[:, :], in_=m[:, :], compare_op=ALU.not_equal, fill=1.0, base=0,
                                   pattern=[[-1, P]], channel_multiplier=1).then_inc(masks_made, 1)
            for m, sign in ((mask_qk, 1), (mask_kq, -1)):
                pool.affine_select(out=m[:, :], in_=m[:, :], compare_op=ALU.is_ge, fill=NEG, base=0,
                                   pattern=[[-sign, P]], channel_multiplier=sign).then_inc(masks_made, 1)
            pool.sem_inc(p2_done, 2 * G)
            pool.sem_inc(p3_done, 2 * G)
            pool.wait_ge(wqkv_in, 16)
            for k in range(KT // 2):
                pool.wait_ge(w_hi_done, k + 1)
                pool.tensor_tensor(wqkv_lo[:, k, :], wqkv_raw[:, k, :], wqkv_hi[:, k, :].bitcast(F32),
                                   ALU.subtract).then_inc(w_split, 1)
            with pool.Fori(0, B) as b:
                def parts(g):
                    for c in range(2):
                        n = 2 * g + c
                        wait_apart(pool, apart["pool"], dve_read, rounds(b, DVE_READS, dve_reads(TILE_AT["QK"[c], g])))
                        pool.tensor_copy(part[:, c, 1, :], rest[:, c, :]).then_inc(p2_done, 1)
                        pool.wait_ge(p2_done, rounds(b, 2 * G, n + 1))
                        pool.tensor_tensor(part[:, c, 2, :], rest[:, c, :], part[:, c, 1, :], ALU.subtract).then_inc(p3_done, 1)

                inverse_deviation(pool, apart["pool"], mv, rstd, minus_half, moments_ready, var_ready, rstd_ready, b + 1)
                for g in range(G):
                    parts(g)

        @block.scalar
        def _(act):
            act.sem_inc(act_read, ACT_READS)
            act.sem_inc(exp_done, UNITS)
            act.sem_inc(attn_hi, G)
            act.wait_ge(wqkv_in, 16)
            for k in range(KT):
                act.copy(wqkv_hi[:, k, :], wqkv_raw[:, k, :]).then_inc(w_hi_done, 1)
            act.wait_ge(wproj_in, 16)
            act.copy(wproj_hi[:, :, :], wproj_raw).then_inc(w_hi_done, 1)
            act.wait_ge(consts_in, 64)
            act.wait_ge(w_split, KT // 2)
            act.wait_ge(setup_done, 1)
            with act.Fori(0, B) as b:
                def done(kind, i):
                    n = TILE_AT[kind, i]
                    act.wait_ge(tile_done, rounds(b, NT, n + 1))
                    return bank[DENSE_BANKS[n % 4]]

                def first_parts(g):
                    for c, kind in enumerate("QK"):
                        src = done(kind, g)
                        act.wait_ge(parts_stored[c], rounds(b, G * 16, g * 16))
                        act.activation(part[:, c, 0, :], src[:, :], ACT.Identity,
                                       bias=bias_qkv[:, c * G + g:c * G + g + 1]).then_inc(act_read, 1)

                def exps(g):
                    for h in range(g * HG, (g + 1) * HG):
                        act.wait_ge(pv_done, rounds(b, NQ, (h - PT_RING) // 4 + 1))
                        for k in range(3):
                            act.wait_ge(t_done, rounds(b, UNITS, 3 * h + k + 1))
                            act.activation(pt[:, h % PT_RING, COL0[k]:COL0[k] + WIDE[k]], bank[3 + k][:, 0:WIDE[k]],
                                           ACT.Exp, scale=1.0 / HD).then_inc(exp_done, 1)

                for k in range(KT):
                    act.copy(fT_hi[:, k, :], done("T", k)[:, :]).then_inc(act_read, 1)
                first_parts(0)
                first_parts(1)
                for t in range(TT):
                    act.copy(v_nat[:, t, :, 0:HD],
                             done("V", t)[:, :].rearrange("p (h e) -> p h e", e=HD)).then_inc(act_read, 1)
                exps(0)
                first_parts(2)
                exps(1)
                first_parts(3)
                exps(2)
                exps(3)
                for g in range(G):
                    for q in range(QUADS):
                        act.wait_ge(on_moved[q], rounds(b, G * 64, (g + 1) * 64))
                    act.activation(fT_hi[:, g, :], attnT[:, g, :], ACT.Identity,
                                   bias=bias_qkv[:, 2 * G + g:2 * G + g + 1]).then_inc(attn_hi, 1)

        @block.vector
        def _(dve):
            for s, n in ((step_done, STEPS), (normed, 1), (dve_read, DVE_READS), (s_maxed, UNITS), (m_ready, G),
                         (pv_read, NQ), (attn_split, G), (x1_ready, TT)):
                dve.sem_inc(s, n)
            dve.wait_ge(consts_in, 64)
            dve.tensor_copy(qx_sb[:, :], qx_raw).then_inc(slopes_cast, 1)
            for s in range(2):
                for h in range(HG):
                    last = dve.tensor_copy(k_st[ROW_X:K_EXP, s, h, :], kx_raw)
            for k in range(KT // 2, KT):
                dve.wait_ge(w_hi_done, k + 1)
                dve.tensor_tensor(wqkv_lo[:, k, :], wqkv_raw[:, k, :], wqkv_hi[:, k, :].bitcast(F32), ALU.subtract)
            dve.wait_ge(w_hi_done, KT + 1)
            dve.tensor_tensor(wproj_lo[:, :, :], wproj_raw, wproj_hi[:, :, :].bitcast(F32),
                              ALU.subtract).then_inc(w_split_v, 1)
            dve.wait_ge(w_split_v, 1)
            dve.memset(v_nat[:, :, :, HD:2 * HD], 1.0).then_inc(setup_done, 1)
            dve.wait_ge(setup_done, 1)
            with dve.Fori(0, B) as b:
                steps = [0]

                def step(ins):
                    steps[0] += 1
                    ins.then_inc(step_done, 1)
                    wait_apart(dve, apart["dve"], step_done, rounds(b, STEPS, steps[0]))

                def done(kind, i):
                    n = TILE_AT[kind, i]
                    dve.wait_ge(tile_done, rounds(b, NT, n + 1))
                    if kind in BY_ACT:
                        dve.wait_ge(act_read, rounds(b, ACT_READS, act_reads(n)))
                    return bank[DENSE_BANKS[n % 4]]

                def remainders(g):
                    for c, kind in enumerate("QK"):
                        src = done(kind, g)
                        dve.wait_ge(p3_done, rounds(b, 2 * G, 2 * g + c - 1))
                        dve.scalar_tensor_tensor(out=rest[:, c, :], in0=src[:, :],
                                                 scalar=bias_qkv[:, c * G + g:c * G + g + 1], in1=part[:, c, 0, :],
                                                 op0=ALU.add, op1=ALU.subtract).then_inc(dve_read, 1)

                def maxima(g, heads):
                    for h in heads:
                        for k in range(3):
                            u = 3 * (g * HG + h) + k
                            dve.wait_ge(s_done, rounds(b, UNITS, u + 1))
                            dve.tensor_reduce(bm[:, h, COL0[k] // P:(COL0[k] + WIDE[k]) // P],
                                              bank[k][:, 0:WIDE[k]].rearrange("p (n q) -> p n q", q=P), AX.X,
                                              ALU.max).then_inc(s_maxed, 1)

                def row_maxima(g):
                    dve.wait_ge(s_maxed, rounds(b, UNITS, HU * (g + 1)))
                    dve.tensor_reduce(mx[:, :, 3], bm[:, :, 0:4], AX.X, ALU.max)
                    dve.tensor_reduce(mx[:, :, 2], bm[:, :, 4:7], AX.X, ALU.max)
                    dve.tensor_copy(mx[:, :, 0], bm[:, :, 7])
                    step(dve.tensor_reduce(mx[:, :, 1], bm[:, :, 8:10], AX.X, ALU.max))
                    flat = mx[:, :, :].rearrange("p h t -> p (h t)")
                    step(dve.tensor_scalar(mparts[:, 0, :], flat, -1.0, None, ALU.mult))
                    dve.scalar_tensor_tensor(out=mparts[:, 1, :], in0=flat, scalar=-1.0, in1=mparts[:, 0, :],
                                             op0=ALU.mult, op1=ALU.subtract).then_inc(m_ready, 1)

                def copy_maxima(g):
                    src = done("M", g)
                    dve.wait_ge(m_placed, rounds(b, G * 32, g * 32))
                    dve.tensor_copy(mt[:, :], src[0:2 * HG * TT, 0:P // 2].bitcast(BF16)).then_inc(dve_read, 1)

                def normalise(g, q):
                    dve.wait_ge(pv_done, rounds(b, NQ, g * QUADS + q + 1))
                    dve.wait_ge(on_moved[q], rounds(b, G * 64, g * 64))
                    step(dve.reciprocal(rden[:, :], bank[6][:, :]))
                    step(dve.stream_shuffle(rden[:, :], rden[:, :], list(range(HD, 2 * HD)) * 2))
                    dve.tensor_tensor(on[:, q, :], bank[6][:, :], rden[:, :], ALU.mult).then_inc(pv_read, 1)

                for t in range(TT):
                    dve.wait_ge(x_in[t], rounds(b, 16, 16))
                layernorm(dve, step, xt, xt, stats, mv, rstd, moments_ready, rstd_ready, b + 1).then_inc(normed, 1)
                for k in range(KT):
                    dve.tensor_tensor(fT_lo[:, k, :], done("T", k)[:, :], fT_hi[:, k, :].bitcast(F32),
                                      ALU.subtract).then_inc(dve_read, 1)
                remainders(0)
                remainders(1)
                maxima(0, range(HG))
                row_maxima(0)
                copy_maxima(0)
                for g in range(G):
                    normalise(g, 0)
                    if g + 1 < G:
                        maxima(g + 1, range(2))
                    normalise(g, 1)
                    if g + 1 < G:
                        maxima(g + 1, range(2, HG))
                        row_maxima(g + 1)
                        if g + 2 < G:
                            remainders(g + 2)
                        copy_maxima(g + 1)
                for t in range(2):
                    dve.wait_ge(xr_in[t], rounds(b, 32, 16))
                    last = dve.tensor_tensor(xr[:, t, :], xr[:, t, :], bproj[:, :], ALU.add)
                step(last)
                for g in range(G):
                    dve.wait_ge(attn_hi, rounds(b, G, g + 1))
                    dve.scalar_tensor_tensor(out=fT_lo[:, g, :], in0=attnT[:, g, :],
                                             scalar=bias_qkv[:, 2 * G + g:2 * G + g + 1], in1=fT_hi[:, g, :].bitcast(F32),
                                             op0=ALU.add, op1=ALU.subtract).then_inc(attn_split, 1)
                for t in range(TT):
                    if t >= 2:
                        dve.wait_ge(xr_in[t % 2], rounds(b, 32, 32))
                        step(dve.tensor_tensor(xr[:, t % 2, :], xr[:, t % 2, :], bproj[:, :], ALU.add))
                    dve.tensor_tensor(xr[:, t % 2, :], done("P", t)[:, :], xr[:, t % 2, :], ALU.add).then_inc(dve_read, 1)
                    dve.wait_ge(dve_read, rounds(b, DVE_READS, dve_reads(TILE_AT["P", t])))
                    dve.sem_inc(x1_ready, 1)
                assert steps[0] == STEPS, steps[0]

        @block.tensor
        def _(pe):
            for s, n in ((tile_done, NT), (s_done, UNITS), (t_done, UNITS), (pv_done, NQ)):
                pe.sem_inc(s, n)
            pe.wait_ge(masks_made, 4)
            pe.wait_ge(w_hi_done, KT + 1)
            pe.wait_ge(w_split, KT // 2)
            pe.wait_ge(setup_done, 1)
            with pe.Fori(0, B) as b:
                def free(kind, i):
                    n = TILE_AT[kind, i]
                    back, m = (b, n - 4) if n >= 4 else (b - 1, NT + n - 4)
                    pe.wait_ge(act_read, rounds(back, ACT_READS, act_reads(m)))
                    pe.wait_ge(dve_read, rounds(back, DVE_READS, dve_reads(m)))
                    return bank[DENSE_BANKS[n % 4]]

                def transpose_tokens():
                    pe.wait_ge(normed, rounds(b, 1, 1))
                    for k in range(KT):
                        out = free("T", k)
                        for t in range(TT):
                            last = pe.transpose(out[:, t * P:(t + 1) * P], xt[:, t, k * P:(k + 1) * P], ident[:, :])
                        last.then_inc(tile_done, 1)

                def project_qk(g):
                    if g == 0:
                        pe.wait_ge(dve_read, rounds(b, DVE_READS, KT))
                    for c, kind in enumerate("QK"):
                        out = free(kind, g)
                        at = c * D + g * P
                        exact_product(pe, out, [(wqkv_hi[:, k, at:at + P], wqkv_lo[:, k, at:at + P],
                                                 fT_hi[:, k, :], fT_lo[:, k, :]) for k in range(KT)]).then_inc(tile_done, 1)

                def project_v():
                    for t in range(TT):
                        out = free("V", t)
                        exact_product(pe, out, [(fT_hi[:, k, t * P:(t + 1) * P], fT_lo[:, k, t * P:(t + 1) * P],
                                                 wqkv_hi[:, k, 2 * D:3 * D], wqkv_lo[:, k, 2 * D:3 * D])
                                                for k in range(KT)]).then_inc(tile_done, 1)

                def score_rows(g, heads):
                    s = g % 2
                    pe.wait_ge(stacked[s], rounds(b, G // 2 * STACK_DMAS * 16, (g // 2 + 1) * STACK_DMAS * 16))
                    for h in heads:
                        for k, tiles in enumerate(((3,), (2, 0), (1,))):
                            u = 3 * (g * HG + h) + k
                            pe.wait_ge(s_maxed, rounds(b, UNITS, u - 2))
                            at = 0
                            for t in tiles:
                                n = (t + 1) * P
                                pe.matmul(bank[k][:, at:at + n], q_st[0:K_MAX, s, h, t * P:(t + 1) * P],
                                          k_st[0:K_MAX, s, h, 0:n], start=True, stop=False)
                                last = pe.matmul(bank[k][:, at + n - P:at + n], identb[:, :], mask_qk[:, :],
                                                 start=False, stop=True)
                                at += n
                            last.then_inc(s_done, 1)

                def transpose_maxima(g):
                    out = free("M", g)
                    wait_apart(pe, apart["pe"], m_ready, rounds(b, G, g + 1))
                    pe.transpose(out[0:2 * HG * TT, 0:P // 2].bitcast(BF16),
                                 mparts[:, :, :].rearrange("p a n -> p (a n)"), identb[:, :]).then_inc(tile_done, 1)

                def exp_scores(g, heads):
                    s = g % 2
                    for h in heads:
                        for k, tiles in enumerate(((0,), (1, 3), (2,))):
                            u = 3 * (g * HG + h) + k
                            pe.wait_ge(exp_done, rounds(b, UNITS, u - 2))
                            at = 0
                            for t in tiles:
                                n = S - t * P
                                pe.matmul(bank[3 + k][:, at:at + n], k_st[0:K_EXP, s, h, t * P:(t + 1) * P],
                                          q_st[0:K_EXP, s, h, t * P:S], start=True, stop=False)
                                last = pe.matmul(bank[3 + k][:, at:at + P], identb[:, :], mask_kq[:, :],
                                                 start=False, stop=True)
                                at += n
                            last.then_inc(t_done, 1)

                def weigh_values(g, q):
                    h0 = g * HG + 4 * q
                    pe.wait_ge(exp_done, rounds(b, UNITS, 3 * (h0 + 4)))
                    pe.wait_ge(pv_read, rounds(b, NQ, g * QUADS + q))
                    for t, at in ((0, 0), (1, 4 * P), (2, 8 * P), (3, 7 * P)):
                        n = S - t * P
                        for j in range(4):
                            last = pe.matmul(bank[6][32 * j:32 * j + 32, t * P:S], v_nat[:, t, h0 + j, :],
                                             pt[:, (h0 + j) % PT_RING, at:at + n], start=(t == 0), stop=(t == TT - 1))
                    last.then_inc(pv_done, 1)

                def attend(g):
                    m = TILE_AT["M", g]
                    pe.wait_ge(act_read, rounds(b, ACT_READS, act_reads(m)))
                    pe.wait_ge(dve_read, rounds(b, DVE_READS, dve_reads(m)))
                    pe.wait_ge(m_placed, rounds(b, G * 32, (g + 1) * 32))
                    exp_scores(g, range(PT_RING))
                    weigh_values(g, 0)
                    exp_scores(g, range(PT_RING, HG))

                def project_out():
                    for t in range(TT):
                        if t == 0:
                            pe.wait_ge(attn_split, rounds(b, G, G))
                        out = free("P", t)
                        exact_product(pe, out, [(fT_hi[:, k, t * P:(t + 1) * P], fT_lo[:, k, t * P:(t + 1) * P],
                                                 wproj_hi[:, k, :], wproj_lo[:, k, :])
                                                for k in range(KT)]).then_inc(tile_done, 1)

                transpose_tokens()
                project_qk(0)
                project_qk(1)
                score_rows(0, range(HG))
                project_v()
                transpose_maxima(0)
                for g in range(G):
                    attend(g)
                    if g + 1 < G:
                        score_rows(g + 1, range(2))
                    weigh_values(g, 1)
                    if g + 1 < G:
                        score_rows(g + 1, range(2, HG))
                        if g + 2 < G:
                            project_qk(g + 2)
                        transpose_maxima(g + 1)
                project_out()


def exact_product(pe, out, operands):
    passes = [p for a_hi, a_lo, b_hi, b_lo in operands for p in ((a_hi, b_hi), (a_hi, b_lo), (a_lo, b_hi))]
    for i, (a, c) in enumerate(passes):
        last = pe.matmul(out[:, :], a, c, start=(i == 0), stop=(i == len(passes) - 1))
    return last


def ffn(nc, x1_dram, wgu_d, wd_d, out_d, bank, ident, minus_half):
    out_v = out_d.rearrange("b (t p) d -> b t p d", p=P)
    RAW = 2

    with ExitStack() as ctx:
        def sb(name, shape, dt=F32):
            return ctx.enter_context(nc.sbuf_tensor(name, shape, dt))

        def sem(name):
            return ctx.enter_context(nc.semaphore(name))

        wgu_hi = sb("wgu_hi", [P, FT, 2, KT, P], F32R)
        wgu_lo = sb("wgu_lo", [P, FT, 2, KT, P], F32R)
        wd_hi = sb("wd_hi", [P, FT, D], F32R)
        wd_lo = sb("wd_lo", [P, FT, D], F32R)
        wgu_raw = sb("wgu_raw", [P, RAW, 2, KT, P])
        wd_raw = sb("wd_raw", [P, RAW, D])
        x1 = sb("x1", [P, TT, D])
        hn = sb("hn", [P, TT, D])
        stats = sb("stats2", [P, TT, 6])
        mv = sb("mv2", [P, TT, 2])
        rstd = sb("rstd2", [P, TT])
        hT_hi = sb("hT_hi", [P, KT, S], F32R)
        hT_lo = sb("hT_lo", [P, KT, S], F32R)
        silu = sb("silu", [P, 2, S])
        gu = sb("gu", [P, 2, S])
        gu_hi = sb("gu_hi", [P, 2, S], F32R)
        gu_lo = sb("gu_lo", [P, 2, S], F32R)

        w_in = [sem(f"w_in{s}") for s in range(RAW)]
        w_hi_done = sem("w_hi_done2")
        w_lo_done = sem("w_lo_done2")
        x1_in = sem("x1_in")
        step_done = sem("step_done2")
        apart = {e: sem(f"apart2_{e}") for e in ("pool", "dve")}
        moments_ready = sem("moments_ready2")
        var_ready = sem("var_ready2")
        rstd_ready = sem("rstd_ready2")
        normed = sem("normed2")
        t_done = sem("t_done2")
        hi_done = sem("hi_done")
        lo_done = sem("lo_done")
        gate_done = sem("gate_done")
        up_done = sem("up_done")
        silu_done = sem("silu_done")
        gu_done = sem("gu_done")
        gu_hi_done = sem("gu_hi_done")
        gu_lo_done = sem("gu_lo_done")
        down_done = sem("down_done")
        out_ready = sem("out_ready")
        out_stored = sem("out_stored")
        block = ctx.enter_context(nc.Block())
        FSTEPS = 1

        @block.sync
        def _(sp):
            for f in range(FT):
                if f >= RAW:
                    sp.wait_ge(w_lo_done, f - RAW + 1)
                sp.dma_start(wgu_raw[:, f % RAW, :, :, :], wgu_d[f]).then_inc(w_in[f % RAW], 16)
                sp.dma_start(wd_raw[:, f % RAW, :], wd_d[f]).then_inc(w_in[f % RAW], 16)

        @block.gpsimd
        def _(pool):
            with pool.Fori(0, B) as b:
                for t in range(TT):
                    pool.dma_start(x1[:, t, :], x1_dram[b, t]).then_inc(x1_in, 16)
                inverse_deviation(pool, apart["pool"], mv, rstd, minus_half, moments_ready, var_ready, rstd_ready, b + 1)
                for t in range(TT):
                    wait_apart(pool, apart["pool"], out_ready, rounds(b, TT, t + 1))
                    pool.dma_start(out_v[b, t], x1[:, t, :]).then_inc(out_stored, 16)
                wait_apart(pool, apart["pool"], out_stored, (b + 1) * 16 * TT)

        @block.scalar
        def _(act):
            for s, n in ((hi_done, KT), (silu_done, FT), (gu_hi_done, FT)):
                act.sem_inc(s, n)

            def weight_hi(f):
                act.wait_ge(w_in[f % RAW], 32 * (f // RAW + 1))
                act.copy(wgu_hi[:, f, :, :, :], wgu_raw[:, f % RAW, :, :, :])
                act.copy(wd_hi[:, f, :], wd_raw[:, f % RAW, :]).then_inc(w_hi_done, 1)

            for f in range(FT):
                weight_hi(f)
            with act.Fori(0, B) as b:
                for k in range(KT):
                    act.wait_ge(t_done, rounds(b, KT, k + 1))
                    act.copy(hT_hi[:, k, :], bank[4 + k][:, :]).then_inc(hi_done, 1)

                def gate(f):
                    act.wait_ge(gate_done, rounds(b, FT, f + 1))
                    act.wait_ge(gu_done, rounds(b, FT, f - 1))
                    act.activation(silu[:, f % 2, :], bank[4 + 2 * (f % 2)][:, :], ACT.Silu).then_inc(silu_done, 1)

                def high(f):
                    act.wait_ge(gu_done, rounds(b, FT, f + 1))
                    act.wait_ge(down_done, rounds(b, FT, f - 1))
                    act.copy(gu_hi[:, f % 2, :], gu[:, f % 2, :]).then_inc(gu_hi_done, 1)

                gate(0)
                for f in range(1, FT):
                    high(f - 1)
                    gate(f)
                high(FT - 1)

        @block.vector
        def _(dve):
            for s, n in ((step_done, FSTEPS), (normed, 1), (lo_done, KT), (gu_done, FT), (gu_lo_done, FT), (out_ready, TT)):
                dve.sem_inc(s, n)
            for f in range(FT):
                dve.wait_ge(w_hi_done, f + 1)
                dve.tensor_tensor(wgu_lo[:, f, :, :, :].rearrange("p c k n -> p (c k n)"),
                                  wgu_raw[:, f % RAW, :, :, :].rearrange("p c k n -> p (c k n)"),
                                  wgu_hi[:, f, :, :, :].rearrange("p c k n -> p (c k n)").bitcast(F32), ALU.subtract)
                dve.tensor_tensor(wd_lo[:, f, :], wd_raw[:, f % RAW, :], wd_hi[:, f, :].bitcast(F32),
                                  ALU.subtract).then_inc(w_lo_done, 1)
            with dve.Fori(0, B) as b:
                steps = [0]

                def step(ins):
                    steps[0] += 1
                    ins.then_inc(step_done, 1)
                    wait_apart(dve, apart["dve"], step_done, rounds(b, FSTEPS, steps[0]))

                dve.wait_ge(x1_in, (b + 1) * 16 * TT)
                layernorm(dve, step, x1, hn, stats, mv, rstd, moments_ready, rstd_ready, b + 1).then_inc(normed, 1)
                for k in range(KT):
                    dve.wait_ge(hi_done, rounds(b, KT, k + 1))
                    dve.tensor_tensor(hT_lo[:, k, :], bank[4 + k][:, :], hT_hi[:, k, :].bitcast(F32),
                                      ALU.subtract).then_inc(lo_done, 1)
                for f in range(FT):
                    dve.wait_ge(silu_done, rounds(b, FT, f + 1))
                    dve.wait_ge(up_done, rounds(b, FT, f + 1))
                    dve.wait_ge(gu_hi_done, rounds(b, FT, f - 1))
                    dve.tensor_tensor(gu[:, f % 2, :], bank[5 + 2 * (f % 2)][:, :], silu[:, f % 2, :],
                                      ALU.mult).then_inc(gu_done, 1)
                    dve.wait_ge(gu_hi_done, rounds(b, FT, f + 1))
                    dve.tensor_tensor(gu_lo[:, f % 2, :], gu[:, f % 2, :], gu_hi[:, f % 2, :].bitcast(F32),
                                      ALU.subtract).then_inc(gu_lo_done, 1)
                dve.wait_ge(down_done, rounds(b, FT, FT))
                for t in range(TT):
                    dve.tensor_tensor(x1[:, t, :], bank[t][:, :], x1[:, t, :], ALU.add).then_inc(out_ready, 1)
                assert steps[0] == FSTEPS

        @block.tensor
        def _(pe):
            for s, n in ((t_done, KT), (gate_done, FT), (up_done, FT), (down_done, FT)):
                pe.sem_inc(s, n)
            with pe.Fori(0, B) as b:
                pe.wait_ge(normed, rounds(b, 1, 1))
                pe.wait_ge(gu_done, rounds(b - 1, FT, FT))
                for k in range(KT):
                    for t in range(TT):
                        last = pe.transpose(bank[4 + k][:, t * P:(t + 1) * P], hn[:, t, k * P:(k + 1) * P], ident[:, :])
                    last.then_inc(t_done, 1)

                def gate_up(f):
                    if f < 2:
                        pe.wait_ge(lo_done, rounds(b, KT, KT))
                    pe.wait_ge(w_lo_done, f + 1)
                    for c, done in enumerate((gate_done, up_done)):
                        pe.wait_ge(gu_done, rounds(b, FT, f - 1))
                        exact_product(pe, bank[4 + 2 * (f % 2) + c],
                                      [(wgu_hi[:, f, c, k, :], wgu_lo[:, f, c, k, :], hT_hi[:, k, :], hT_lo[:, k, :])
                                       for k in range(KT)]).then_inc(done, 1)

                def down(f):
                    if f == 0:
                        pe.wait_ge(out_ready, rounds(b - 1, TT, TT))
                    pe.wait_ge(gu_lo_done, rounds(b, FT, f + 1))
                    for t in range(TT):
                        cols = slice(t * P, (t + 1) * P)
                        for i, (a, w) in enumerate(((gu_hi, wd_hi), (gu_hi, wd_lo), (gu_lo, wd_hi))):
                            last = pe.matmul(bank[t][:, :], a[:, f % 2, cols], w[:, f, :],
                                             start=(f == 0 and i == 0), stop=(f == FT - 1 and i == 2))
                    last.then_inc(down_done, 1)

                gate_up(0)
                for f in range(1, FT):
                    gate_up(f)
                    down(f - 1)
                down(FT - 1)


def kernel(**inputs):
    from concourse import bacc
    from concourse.bass_utils import run_bass_kernel_spmd

    def given(name):
        return np.ascontiguousarray(inputs["L0_" + name])

    def padded(w):
        return np.concatenate([w, np.zeros((FT * P - F, D), w.dtype)])

    both = np.stack([padded(given("ffn_w_gate")), padded(given("ffn_w_up"))])
    wgu = np.ascontiguousarray(both.reshape(2, FT, P, KT, P).transpose(1, 4, 0, 3, 2))
    wd = np.ascontiguousarray(padded(given("ffn_w_down").T).reshape(FT, P, D))
    q_rows, k_rows = extra_rows()
    arrays = {
        "x": given("attn_hidden_states"), "w_qkv": given("attn_w_attn"), "b_qkv": given("attn_b_attn"),
        "w_proj": given("attn_w_proj"), "b_proj": given("attn_b_proj"), "w_gate_up": wgu, "w_down": wd,
        "q_rows": q_rows, "k_rows": k_rows,
    }
    nc = bacc.Bacc("TRN2", target_bir_lowering=False, num_devices=1)
    args = [nc.dram_tensor(n, a.shape, mybir.dt.from_np(a.dtype), kind="ExternalInput").ap() for n, a in arrays.items()]
    out = nc.dram_tensor("out", (B, S, D), F32, kind="ExternalOutput").ap()
    kernel_body(nc, *args, out)
    return run_bass_kernel_spmd(nc, [arrays], core_ids=[0]).results[0]["out"]
```

```python
from contextlib import ExitStack

import numpy as np

import concourse.bass as bass
from concourse import mybir

F32 = mybir.dt.float32
F32R = mybir.dt.float32r
BF16 = mybir.dt.bfloat16
ACT = mybir.ActivationFunctionType
ALU = mybir.AluOpType
AX = mybir.AxisListType

P = 128
B, S, D = 4, 512, 512
H, HD = 32, 16
F = 1376
KT = D // P
TT = S // P
HG = P // HD
G = H // HG
NQ = H // 4
QG = NQ // G
SLOTS = 4
FT = (F + P - 1) // P
EPS = 1e-5
NEG = -1e30

Q_TERM = (0, 1, 2, 0, 1, 0)
K_TERM = (0, 0, 0, 1, 1, 2)
TERMS = len(Q_TERM)
ROW_X = TERMS * HD
K_MAX = ROW_X + 1
K_EXP = ROW_X + 5

WIDE = (512, 512, 256)
COL0 = (0, 512, 1024)
NBLK = sum(WIDE) // P
PT_RING = 6

SPREAD = (7, 3, 4, 5)
TILES = ([("T", k) for k in range(KT)] + [("Q", 0), ("K", 0), ("Q", 1), ("K", 1)] + [("V", t) for t in range(TT)]
         + [("M", 0), ("M", 1), ("Q", 2), ("K", 2), ("M", 2), ("M", 3), ("Q", 3), ("K", 3)]
         + [("M", c) for c in range(4, NQ)] + [("P", t) for t in range(TT)])
NT = len(TILES)
TILE_AT = {t: n for n, t in enumerate(TILES)}
PROLOGUE = TILE_AT["V", TT - 1] + 1
TILE_BANK = [SPREAD[n % 4] if n < PROLOGUE else SPREAD[i] if kind == "P" else 7 for n, (kind, i) in enumerate(TILES)]
BY_ACT = "TQKV"
BY_DVE = "TQKMP"


def act_reads(n):
    return sum(kind in BY_ACT for kind, _ in TILES[:n + 1])


def dve_reads(n):
    return sum(kind in BY_DVE for kind, _ in TILES[:n + 1])


def before_in_bank(n):
    earlier = [m for m in range(n) if TILE_BANK[m] == TILE_BANK[n]]
    return (0, earlier[-1]) if earlier else (1, max(m for m in range(NT) if TILE_BANK[m] == TILE_BANK[n]))


ACT_READS, DVE_READS = act_reads(NT - 1), dve_reads(NT - 1)
STEPS = 1 + 2 * NQ + G + 3


def slopes():
    start = 2.0 ** (-(2.0 ** -(np.log2(H) - 3)))
    return (start ** np.arange(1, H + 1, dtype=np.float32)).astype(np.float32)


def bf16_part(x):
    return (x.view(np.uint32) & np.uint32(0xFFFF0000)).view(np.float32)


def extra_rows():
    s, parts = slopes() * np.float32(HD), []
    for _ in range(3):
        p = bf16_part(s)
        parts.append(np.repeat(p[:, None], S, 1))
        s = s - p
    pos = np.arange(S, dtype=np.float32) - S // 2
    one = np.ones(S, np.float32)
    return np.concatenate(parts), np.stack([pos, one, pos, one, pos])


def rounds(b, per, k=0):
    return (b + 1) * per + k


def wait_apart(eng, apart, semaphore, value):
    eng.wait_ge(semaphore, value)
    eng.sem_inc(apart, 1)


def layernorm(dve, step, src, dst, stats, mv, rstd, moments_ready, rstd_ready, count):
    for t in range(TT):
        last = dve.bn_stats(stats[:, t, :], src[:, t, :])
    step(last)
    for t in range(TT):
        last = dve.bn_aggr(mv[:, t, :], stats[:, t, :])
    last.then_inc(moments_ready, 1)
    dve.wait_ge(moments_ready, count)
    dve.wait_ge(rstd_ready, count)
    for t in range(TT):
        last = dve.tensor_scalar(dst[:, t, :], src[:, t, :], mv[:, t, 0:1], rstd[:, t:t + 1], ALU.subtract, ALU.mult)
    return last


def inverse_deviation(pool, apart, mv, rstd, minus_half, moments_ready, var_ready, rstd_ready, count):
    wait_apart(pool, apart, moments_ready, count)
    pool.tensor_scalar(mv[:, :, 1], mv[:, :, 1], EPS, None, ALU.add).then_inc(var_ready, 1)
    pool.wait_ge(var_ready, count)
    pool.tensor_tensor(rstd[:, :], mv[:, :, 1], minus_half[:, :], ALU.pow).then_inc(rstd_ready, 1)


def kernel_body(nc, x_d, wqkv_d, bqkv_d, wproj_d, bproj_d, wgu_d, wd_d, qx_d, kx_d, out_d):
    with ExitStack() as whole:
        bank = [whole.enter_context(nc.psum_tensor(f"bank{i}", [P, 512], F32)) for i in range(8)]
        ident = whole.enter_context(nc.sbuf_tensor("ident", [P, P], F32))
        minus_half = whole.enter_context(nc.sbuf_tensor("minus_half", [P, TT], F32))
        x1_dram = nc.dram_tensor("x1_dram", [B, TT, P, D], F32, kind="Internal").ap()
        attention(nc, x_d, wqkv_d, bqkv_d, wproj_d, bproj_d, qx_d, kx_d, x1_dram, bank, ident, minus_half)
        ffn(nc, x1_dram, wgu_d, wd_d, out_d, bank, ident, minus_half)


def attention(nc, x_d, wqkv_d, bqkv_d, wproj_d, bproj_d, qx_d, kx_d, x1_dram, bank, ident, minus_half):
    x_v = x_d.rearrange("b (t p) d -> b t p d", p=P)
    stack_dram = nc.dram_tensor("stack_dram", [2, G, TERMS, P, S], BF16, kind="Internal").ap()
    slopes_dram = nc.dram_tensor("slopes_dram", [3, H, S], BF16, kind="Internal").ap()
    pv_dram = nc.dram_tensor("pv_dram", [G, QG * P, S], F32, kind="Internal").ap()

    with ExitStack() as ctx:
        def sb(name, shape, dt=F32):
            return ctx.enter_context(nc.sbuf_tensor(name, shape, dt))

        def sem(name):
            return ctx.enter_context(nc.semaphore(name))

        wqkv_hi = sb("wqkv_hi", [P, KT, 3 * D], F32R)
        wqkv_lo = sb("wqkv_lo", [P, KT, 3 * D], F32R)
        wproj_hi = sb("wproj_hi", [P, KT, D], F32R)
        wproj_lo = sb("wproj_lo", [P, KT, D], F32R)
        bias_qkv = sb("bias_qkv", [P, 3 * G])
        bproj = sb("bproj", [P, D])
        identb = sb("identb", [P, P], BF16)
        mask_qk = sb("mask_qk", [P, P], BF16)
        mask_kq = sb("mask_kq", [P, P], BF16)
        xt = sb("xt", [P, TT, D])
        stats = sb("stats", [P, TT, 6])
        mv = sb("mv", [P, TT, 2])
        rstd = sb("rstd", [P, TT])
        fT_hi = sb("fT_hi", [P, KT, S], F32R)
        fT_lo = sb("fT_lo", [P, KT, S], F32R)
        part = sb("part", [P, 2, 3, S], BF16)
        rest = sb("rest", [P, 2, S])
        q_st = sb("q_st", [P, SLOTS, 4, S], BF16)
        k_st = sb("k_st", [P, SLOTS, 4, S], BF16)
        pt = sb("pt", [P, PT_RING, NBLK * P])
        v_nat = sb("v_nat", [P, TT, H, 2 * HD])
        bm = sb("bm", [P, 4, NBLK])
        mx = sb("mx", [P, 4, TT])
        mparts = sb("mparts", [P, 2, 4 * TT], BF16)
        mt = sb("mt", [2 * 4 * TT, 2, P], BF16)
        pv_raw = sb("pv_raw", [P, 2, S])
        attnT = sb("attnT", [P, 2, S])
        sums = sb("sums", [P, 2, S])
        xr = sb("xr", [P, 2, D])
        qx_sb = sb("qx_sb", [3 * H, S], BF16)
        wqkv_raw = pt[:, :, :].rearrange("p a b -> p (a b)")[:, 0:KT * 3 * D].rearrange("p (k n) -> p k n", k=KT)
        wproj_raw = v_nat[:, :, :, :].rearrange("p t h e -> p (t h e)")[:, 0:KT * D].rearrange("p (k n) -> p k n", k=KT)
        qx_raw = attnT[0:3 * H, 0, :]
        kx_raw = pv_raw[ROW_X:K_EXP, 0, :]

        consts_in = sem("consts_in")
        wqkv_in = [sem(f"wqkv_in{k}") for k in range(KT)]
        wproj_in = sem("wproj_in")
        zeroed = sem("zeroed")
        masks_made = sem("masks_made")
        w_hi_done = sem("w_hi_done")
        w_split = sem("w_split")
        w_split_v = sem("w_split_v")
        setup_done = sem("setup_done")
        slopes_cast = sem("slopes_cast")
        slopes_stored = sem("slopes_stored")
        x_in = [sem(f"x_in{t}") for t in range(TT)]
        apart = {e: sem(f"apart_{e}") for e in ("sp", "pool", "dve", "pe")}
        step_done = sem("step_done")
        moments_ready = sem("moments_ready")
        var_ready = sem("var_ready")
        rstd_ready = sem("rstd_ready")
        normed = sem("normed")
        tile_done = sem("tile_done")
        act_read = sem("act_read")
        dve_read = sem("dve_read")
        p2_done = sem("p2_done")
        p3_done = sem("p3_done")
        parts_stored = [sem("q_stored"), sem("k_stored")]
        stacked = [sem(f"stacked{s}") for s in range(SLOTS)]
        s_done = sem("s_done")
        s_maxed = sem("s_maxed")
        m_ready = sem("m_ready")
        m_placed = [sem(f"m_placed{i}") for i in range(2)]
        t_done = sem("t_done")
        exp_done = sem("exp_done")
        pv_done = sem("pv_done")
        pv_copied = sem("pv_copied")
        pv_stored = [sem(f"pv_stored{i}") for i in range(2)]
        attn_in = [sem(f"attn_in{i}") for i in range(2)]
        attn_ready = sem("attn_ready")
        attn_hi = sem("attn_hi")
        attn_split = sem("attn_split")
        xr_in = [sem(f"xr_in{s}") for s in range(2)]
        x1_ready = sem("x1_ready")
        x1_stored = [sem(f"x1_stored{s}") for s in range(2)]
        block = ctx.enter_context(nc.Block())

        UNITS = 3 * H
        QU = 3 * 4
        STACK_INCS = 3 * 16
        PARTS_INCS = 3 * 16

        @block.sync
        def _(sp):
            for t in range(TT):
                sp.dma_start(xt[:, t, :], x_v[0, t]).then_inc(x_in[t], 16)
            for k in range(KT):
                sp.dma_start(wqkv_raw[:, k, :], wqkv_d[k * P:(k + 1) * P, :]).then_inc(wqkv_in[k], 16)
            sp.dma_start(qx_raw, qx_d).then_inc(consts_in, 16)
            sp.dma_start(kx_raw, kx_d).then_inc(consts_in, 16)
            with nc.allow_non_contiguous_dma(reason="biases, once, a column per partition"):
                sp.dma_start(bias_qkv[:, :], bqkv_d.rearrange("(c p) -> p c", p=P)).then_inc(consts_in, 16)
            sp.dma_start(bproj[:, :], bproj_d.rearrange("(a d) -> a d", a=1).broadcast_to([P, D])).then_inc(consts_in, 16)
            sp.dma_start(wproj_raw, wproj_d.rearrange("(k p) n -> p k n", p=P)).then_inc(wproj_in, 16)
            for s, n in ([(x, G * PARTS_INCS) for x in parts_stored] + [(x, NQ // 2 * 32) for x in m_placed]
                         + [(x, NQ // SLOTS * STACK_INCS) for x in stacked] + [(x, NQ // 2 * 16) for x in pv_stored]
                         + [(x, G // 2 * 32) for x in attn_in] + [(x, TT // 2 * 16) for x in xr_in + x1_stored]):
                sp.sem_inc(s, n)
            sp.wait_ge(slopes_cast, 1)
            sp.dma_start(slopes_dram.rearrange("a h s -> (a h) s"), qx_sb[:, :]).then_inc(slopes_stored, 16)
            sp.wait_ge(slopes_stored, 16)
            sp.wait_ge(setup_done, 1)
            with sp.Fori(0, B) as b:
                def load_next_tokens():
                    wait_apart(sp, apart["sp"], tile_done, rounds(b, NT, KT))
                    for t in range(TT):
                        sp.dma_start(xt[:, t, :], x_v[(b + 1) % B, t]).then_inc(x_in[t], 16)

                def store_parts(g):
                    q_parts, k_parts = part[:, 0, :, :], part[:, 1, :, :]
                    sources = ((q_parts[:, 0:3, :], q_parts[:, 0:2, :], q_parts[:, 0:1, :]),
                               [k_parts[:, i:i + 1, :].broadcast_to([P, n, S]) for i, n in enumerate((3, 2, 1))])
                    for c in range(2):
                        sp.wait_ge(p3_done, rounds(b, 2 * G, 2 * g + c + 1))
                        for r, n, src in zip((0, 3, 5), (3, 2, 1), sources[c]):
                            sp.dma_start(stack_dram[c, g, r:r + n].rearrange("r p s -> p r s"), src).then_inc(parts_stored[c], 16)

                def load_stacks(c):
                    g, at, s = c // QG, c % QG * 4, c % SLOTS
                    wait_apart(sp, apart["sp"], t_done, rounds(b, UNITS, QU * (c + 1 - SLOTS)))
                    for i, st in enumerate((q_st, k_st)):
                        sp.wait_ge(parts_stored[i], rounds(b, G * PARTS_INCS, (g + 1) * PARTS_INCS))
                        sp.dma_start(st[0:ROW_X, s, :, :], stack_dram[i, g].rearrange("r (e h) s -> (r e) h s", h=HG)
                                     [:, at:at + 4, :]).then_inc(stacked[s], 16)
                    sp.dma_start(q_st[ROW_X:K_EXP:2, s, :, :], slopes_dram[:, 4 * c:4 * c + 4, :]).then_inc(stacked[s], 16)

                def place_maxima(c):
                    n = 4 * TT
                    sp.wait_ge(dve_read, rounds(b, DVE_READS, dve_reads(TILE_AT["M", c])))
                    for a in range(2):
                        row = ROW_X + 1 + 2 * a
                        sp.dma_start(q_st[row:row + 1, c % SLOTS, :, :].rearrange("p h (t n) -> p (h t) n", n=P),
                                     mt[a * n:(a + 1) * n, c % 2, :]).then_inc(m_placed[c % 2], 16)

                def regroup(c):
                    g, at = c // QG, c % QG * P
                    sp.wait_ge(pv_copied, rounds(b, NQ, c + 1))
                    sp.dma_start(pv_dram[g, at:at + P, :], pv_raw[:, c % 2, :]).then_inc(pv_stored[c % 2], 16)
                    if c % QG == QG - 1:
                        wait_apart(sp, apart["sp"], attn_split, rounds(b, G, g - 1))
                        for i in range(2):
                            sp.wait_ge(pv_stored[i], rounds(b, G * 16, (g + 1) * 16))
                        rows = pv_dram[g].rearrange("(h e) s -> h e s", e=2 * HD)
                        sp.dma_start(attnT[:, g % 2, :], rows[:, 0:HD, :]).then_inc(attn_in[g % 2], 16)
                        sp.dma_start(sums[:, g % 2, :], rows[:, HD:2 * HD, :]).then_inc(attn_in[g % 2], 16)

                store_parts(0)
                load_next_tokens()
                load_stacks(0)
                load_stacks(1)
                store_parts(1)
                load_stacks(2)
                load_stacks(3)
                place_maxima(0)
                for c in range(NQ):
                    if c + 1 < NQ:
                        place_maxima(c + 1)
                    if c >= 1:
                        regroup(c - 1)
                    if c in (0, 2):
                        store_parts(2 + c // 2)
                    if c + SLOTS < NQ:
                        load_stacks(c + SLOTS)
                for t in range(2):
                    wait_apart(sp, apart["sp"], x1_stored[t], rounds(b - 1, 32, 32))
                    sp.dma_start(xr[:, t, :], x_v[b, t]).then_inc(xr_in[t], 16)
                regroup(NQ - 1)
                for t in range(TT):
                    wait_apart(sp, apart["sp"], x1_ready, rounds(b, TT, t + 1))
                    sp.dma_start(x1_dram[b, t], xr[:, t % 2, :]).then_inc(x1_stored[t % 2], 16)
                    if t < 2:
                        wait_apart(sp, apart["sp"], x1_stored[t], rounds(b, 32, 16))
                        sp.dma_start(xr[:, t, :], x_v[b, t + 2]).then_inc(xr_in[t], 16)
            for t in range(2):
                sp.wait_ge(x1_stored[t], rounds(B - 1, 32, 32))
            for t in range(TT):
                sp.wait_ge(x_in[t], 16 * (B + 1))

        @block.gpsimd
        def _(pool):
            for m in (ident, identb, mask_qk, mask_kq):
                pool.memset(m[:, :], 0.0).then_inc(zeroed, 1)
            pool.memset(minus_half[:, :], -0.5).then_inc(zeroed, 1)
            pool.wait_ge(zeroed, 5)
            for m in (ident, identb):
                pool.affine_select(out=m[:, :], in_=m[:, :], compare_op=ALU.not_equal, fill=1.0, base=0,
                                   pattern=[[-1, P]], channel_multiplier=1).then_inc(masks_made, 1)
            for m, sign in ((mask_qk, 1), (mask_kq, -1)):
                pool.affine_select(out=m[:, :], in_=m[:, :], compare_op=ALU.is_ge, fill=NEG, base=0,
                                   pattern=[[-sign, P]], channel_multiplier=sign).then_inc(masks_made, 1)
            pool.sem_inc(p2_done, 2 * G)
            pool.sem_inc(p3_done, 2 * G)
            inverse_deviation(pool, apart["pool"], mv, rstd, minus_half, moments_ready, var_ready, rstd_ready, 1)
            pool.wait_ge(w_hi_done, 1)
            pool.tensor_tensor(wqkv_lo[:, 0, :], wqkv_raw[:, 0, :], wqkv_hi[:, 0, :].bitcast(F32),
                               ALU.subtract).then_inc(w_split, 1)
            with pool.Fori(0, B) as b:
                for g in range(G):
                    for c in range(2):
                        n = 2 * g + c
                        wait_apart(pool, apart["pool"], dve_read, rounds(b, DVE_READS, dve_reads(TILE_AT["QK"[c], g])))
                        pool.tensor_copy(part[:, c, 1, :], rest[:, c, :]).then_inc(p2_done, 1)
                        pool.wait_ge(p2_done, rounds(b, 2 * G, n + 1))
                        pool.tensor_tensor(part[:, c, 2, :], rest[:, c, :], part[:, c, 1, :], ALU.subtract).then_inc(p3_done, 1)
                inverse_deviation(pool, apart["pool"], mv, rstd, minus_half, moments_ready, var_ready, rstd_ready, b + 2)

        @block.scalar
        def _(act):
            act.sem_inc(act_read, ACT_READS)
            act.sem_inc(exp_done, UNITS)
            act.sem_inc(pv_copied, NQ)
            act.sem_inc(attn_hi, G)
            for k in range(KT):
                act.wait_ge(wqkv_in[k], 16)
                act.copy(wqkv_hi[:, k, :], wqkv_raw[:, k, :]).then_inc(w_hi_done, 1)
            act.wait_ge(wproj_in, 16)
            act.copy(wproj_hi[:, :, :], wproj_raw).then_inc(w_hi_done, 1)
            act.wait_ge(consts_in, 64)
            with act.Fori(0, B) as b:
                def done(kind, i):
                    n = TILE_AT[kind, i]
                    act.wait_ge(tile_done, rounds(b, NT, n + 1))
                    return bank[TILE_BANK[n]]

                def first_part(c, g):
                    src = done("QK"[c], g)
                    act.wait_ge(parts_stored[c], rounds(b, G * PARTS_INCS, g * PARTS_INCS))
                    act.activation(part[:, c, 0, :], src[:, :], ACT.Identity,
                                   bias=bias_qkv[:, c * G + g:c * G + g + 1]).then_inc(act_read, 1)

                def exponentials(h):
                    act.wait_ge(pv_done, rounds(b, NQ, (h - PT_RING) // 4 + 1))
                    for k in range(3):
                        act.wait_ge(t_done, rounds(b, UNITS, 3 * h + k + 1))
                        act.activation(pt[:, h % PT_RING, COL0[k]:COL0[k] + WIDE[k]], bank[3 + k][:, 0:WIDE[k]],
                                       ACT.Exp, scale=1.0 / HD).then_inc(exp_done, 1)

                def copy_pv(c):
                    act.wait_ge(pv_done, rounds(b, NQ, c + 1))
                    act.wait_ge(pv_stored[c % 2], rounds(b, G * 16, c // 2 * 16))
                    act.copy(pv_raw[:, c % 2, :], bank[6][:, :]).then_inc(pv_copied, 1)

                def attention_hi(g):
                    if g == 0:
                        act.wait_ge(tile_done, rounds(b, NT, TILE_AT["K", G - 1] + 1))
                    act.wait_ge(attn_ready, rounds(b, G, g + 1))
                    act.activation(fT_hi[:, g, :], attnT[:, g % 2, :], ACT.Identity,
                                   bias=bias_qkv[:, 2 * G + g:2 * G + g + 1]).then_inc(attn_hi, 1)

                for k in range(KT):
                    act.copy(fT_hi[:, k, :], done("T", k)[:, :]).then_inc(act_read, 1)
                for g in range(2):
                    for c in range(2):
                        first_part(c, g)
                act.wait_ge(w_split, 1)
                act.wait_ge(setup_done, 1)
                for t in range(TT):
                    act.copy(v_nat[:, t, :, 0:HD],
                             done("V", t)[:, :].rearrange("p (h e) -> p h e", e=HD)).then_inc(act_read, 1)
                for c in range(NQ):
                    exponentials(4 * c)
                    exponentials(4 * c + 1)
                    if c in (0, 2):
                        first_part(0, 2 + c // 2)
                    exponentials(4 * c + 2)
                    if c >= 1:
                        copy_pv(c - 1)
                    exponentials(4 * c + 3)
                    if c in (0, 2):
                        first_part(1, 2 + c // 2)
                    if c % 2 == 1 and c >= 3:
                        attention_hi((c - 3) // 2)
                copy_pv(NQ - 1)
                attention_hi(G - 1)

        @block.vector
        def _(dve):
            for s, n in ((step_done, STEPS), (dve_read, DVE_READS), (s_maxed, UNITS), (m_ready, NQ),
                         (attn_ready, G), (attn_split, G), (x1_ready, TT)):
                dve.sem_inc(s, n)
            first_steps = [0]

            def first_step(ins):
                first_steps[0] += 1
                ins.then_inc(w_split_v, 1)
                dve.wait_ge(w_split_v, first_steps[0])

            for t in range(TT):
                dve.wait_ge(x_in[t], 16)
            layernorm(dve, first_step, xt, xt, stats, mv, rstd, moments_ready, rstd_ready, 1).then_inc(normed, 1)
            for k in range(1, KT):
                dve.wait_ge(w_hi_done, k + 1)
                first_step(dve.tensor_tensor(wqkv_lo[:, k, :], wqkv_raw[:, k, :], wqkv_hi[:, k, :].bitcast(F32), ALU.subtract))
            assert first_steps[0] == qkv_split_count()
            dve.wait_ge(consts_in, 64)
            dve.tensor_copy(qx_sb[:, :], qx_raw).then_inc(slopes_cast, 1)
            for s in range(SLOTS):
                dve.tensor_copy(k_st[ROW_X:K_EXP, s, :, :], kx_raw.rearrange("p (a s) -> p a s", a=1).broadcast_to([K_EXP - ROW_X, 4, S]))
            dve.wait_ge(w_hi_done, KT + 1)
            first_step(dve.tensor_tensor(wproj_lo[:, :, :], wproj_raw, wproj_hi[:, :, :].bitcast(F32), ALU.subtract))
            dve.memset(v_nat[:, :, :, HD:2 * HD], 1.0).then_inc(setup_done, 1)
            dve.wait_ge(setup_done, 1)
            with dve.Fori(0, B) as b:
                steps = [0]

                def step(ins):
                    steps[0] += 1
                    ins.then_inc(step_done, 1)
                    wait_apart(dve, apart["dve"], step_done, rounds(b, STEPS, steps[0]))

                def done(kind, i):
                    n = TILE_AT[kind, i]
                    dve.wait_ge(tile_done, rounds(b, NT, n + 1))
                    if kind in BY_ACT:
                        dve.wait_ge(act_read, rounds(b, ACT_READS, act_reads(n)))
                    return bank[TILE_BANK[n]]

                def remainder(c, g):
                    src = done("QK"[c], g)
                    dve.wait_ge(p3_done, rounds(b, 2 * G, 2 * g + c - 1))
                    dve.scalar_tensor_tensor(out=rest[:, c, :], in0=src[:, :],
                                             scalar=bias_qkv[:, c * G + g:c * G + g + 1], in1=part[:, c, 0, :],
                                             op0=ALU.add, op1=ALU.subtract).then_inc(dve_read, 1)

                def block_maxima(h):
                    for k in range(3):
                        dve.wait_ge(s_done, rounds(b, UNITS, 3 * h + k + 1))
                        dve.tensor_reduce(bm[:, h % 4, COL0[k] // P:(COL0[k] + WIDE[k]) // P],
                                          bank[k][:, 0:WIDE[k]].rearrange("p (n q) -> p n q", q=P), AX.X,
                                          ALU.max).then_inc(s_maxed, 1)

                def row_maxima(c):
                    dve.wait_ge(s_maxed, rounds(b, UNITS, QU * (c + 1)))
                    dve.tensor_reduce(mx[:, :, 3], bm[:, :, 0:4], AX.X, ALU.max)
                    dve.tensor_reduce(mx[:, :, 2], bm[:, :, 4:7], AX.X, ALU.max)
                    dve.tensor_copy(mx[:, :, 0], bm[:, :, 7])
                    step(dve.tensor_reduce(mx[:, :, 1], bm[:, :, 8:10], AX.X, ALU.max))
                    flat = mx[:, :, :].rearrange("p h t -> p (h t)")
                    step(dve.tensor_scalar(mparts[:, 0, :], flat, -1.0, None, ALU.mult))
                    dve.scalar_tensor_tensor(out=mparts[:, 1, :], in0=flat, scalar=-1.0, in1=mparts[:, 0, :],
                                             op0=ALU.mult, op1=ALU.subtract).then_inc(m_ready, 1)

                def copy_maxima(c):
                    src = done("M", c)
                    dve.wait_ge(m_placed[c % 2], rounds(b, NQ // 2 * 32, c // 2 * 32))
                    dve.tensor_copy(mt[:, c % 2, :], src[0:2 * 4 * TT, 0:P // 2].bitcast(BF16)).then_inc(dve_read, 1)

                def finish_group(g):
                    dve.wait_ge(attn_in[g % 2], rounds(b, G // 2 * 32, (g // 2 + 1) * 32))
                    step(dve.reciprocal(sums[:, g % 2, :], sums[:, g % 2, :]))
                    dve.tensor_tensor(attnT[:, g % 2, :], attnT[:, g % 2, :], sums[:, g % 2, :], ALU.mult).then_inc(attn_ready, 1)
                    dve.wait_ge(attn_hi, rounds(b, G, g + 1))
                    dve.scalar_tensor_tensor(out=fT_lo[:, g, :], in0=attnT[:, g % 2, :],
                                             scalar=bias_qkv[:, 2 * G + g:2 * G + g + 1], in1=fT_hi[:, g, :].bitcast(F32),
                                             op0=ALU.add, op1=ALU.subtract).then_inc(attn_split, 1)

                for k in range(KT):
                    dve.tensor_tensor(fT_lo[:, k, :], done("T", k)[:, :], fT_hi[:, k, :].bitcast(F32),
                                      ALU.subtract).then_inc(dve_read, 1)
                for g in range(2):
                    for c in range(2):
                        remainder(c, g)
                for h in range(4):
                    block_maxima(h)
                row_maxima(0)
                copy_maxima(0)
                for h in range(4, 8):
                    block_maxima(h)
                row_maxima(1)
                for c in range(NQ):
                    for i in range(4):
                        if c + 2 < NQ:
                            block_maxima(4 * (c + 2) + i)
                        if i == 0 and c + 1 < NQ:
                            copy_maxima(c + 1)
                        if i == 1 and c in (0, 2):
                            remainder(0, 2 + c // 2)
                        if i == 3 and c in (0, 2):
                            remainder(1, 2 + c // 2)
                    if c + 2 < NQ:
                        row_maxima(c + 2)
                    if c % 2 == 1 and c >= 3:
                        finish_group((c - 3) // 2)
                    if c == NQ - 2:
                        for t in range(TT):
                            dve.wait_ge(x_in[t], (b + 2) * 16)
                        layernorm(dve, step, xt, xt, stats, mv, rstd, moments_ready, rstd_ready, b + 2).then_inc(normed, 1)
                for t in range(2):
                    dve.wait_ge(xr_in[t], rounds(b, 32, 16))
                    last = dve.tensor_tensor(xr[:, t, :], xr[:, t, :], bproj[:, :], ALU.add)
                step(last)
                finish_group(G - 1)
                for t in range(TT):
                    if t >= 2:
                        dve.wait_ge(xr_in[t % 2], rounds(b, 32, 32))
                        step(dve.tensor_tensor(xr[:, t % 2, :], xr[:, t % 2, :], bproj[:, :], ALU.add))
                    dve.tensor_tensor(xr[:, t % 2, :], done("P", t)[:, :], xr[:, t % 2, :], ALU.add).then_inc(dve_read, 1)
                    dve.wait_ge(dve_read, rounds(b, DVE_READS, dve_reads(TILE_AT["P", t])))
                    dve.sem_inc(x1_ready, 1)
                assert steps[0] == STEPS, (steps[0], STEPS)

        @block.tensor
        def _(pe):
            for s, n in ((tile_done, NT), (s_done, UNITS), (t_done, UNITS), (pv_done, NQ)):
                pe.sem_inc(s, n)
            pe.wait_ge(masks_made, 4)
            with pe.Fori(0, B) as b:
                def free(kind, i):
                    n = TILE_AT[kind, i]
                    back, m = before_in_bank(n)
                    pe.wait_ge(act_read, rounds(b - back, ACT_READS, act_reads(m)))
                    pe.wait_ge(dve_read, rounds(b - back, DVE_READS, dve_reads(m)))
                    return bank[TILE_BANK[n]]

                def transpose_tokens():
                    pe.wait_ge(normed, b + 1)
                    for k in range(KT):
                        out = free("T", k)
                        for t in range(TT):
                            last = pe.transpose(out[:, t * P:(t + 1) * P], xt[:, t, k * P:(k + 1) * P], ident[:, :])
                        last.then_inc(tile_done, 1)

                def project(c, g):
                    if (c, g) == (0, 0):
                        pe.wait_ge(w_split, 1)
                        pe.wait_ge(w_split_v, qkv_split_count())
                        pe.wait_ge(dve_read, rounds(b, DVE_READS, KT))
                    at = c * D + g * P
                    exact_product(pe, free("QK"[c], g), [(wqkv_hi[:, k, at:at + P], wqkv_lo[:, k, at:at + P],
                                                          fT_hi[:, k, :], fT_lo[:, k, :]) for k in range(KT)]).then_inc(tile_done, 1)

                def values(t):
                    exact_product(pe, free("V", t), [(fT_hi[:, k, t * P:(t + 1) * P], fT_lo[:, k, t * P:(t + 1) * P],
                                                      wqkv_hi[:, k, 2 * D:3 * D], wqkv_lo[:, k, 2 * D:3 * D])
                                                     for k in range(KT)]).then_inc(tile_done, 1)

                def scores(h):
                    c, s = h // 4, h // 4 % SLOTS
                    if h % 4 == 0:
                        n = NQ // SLOTS * STACK_INCS
                        pe.wait_ge(stacked[s], rounds(b, n, (c // SLOTS + 1) * STACK_INCS))
                    for k, tiles in enumerate(((3,), (2, 0), (1,))):
                        pe.wait_ge(s_maxed, rounds(b, UNITS, 3 * h + k - 2))
                        at = 0
                        for t in tiles:
                            n = (t + 1) * P
                            pe.matmul(bank[k][:, at:at + n], q_st[0:K_MAX, s, h % 4, t * P:(t + 1) * P],
                                      k_st[0:K_MAX, s, h % 4, 0:n], start=True, stop=False)
                            last = pe.matmul(bank[k][:, at + n - P:at + n], identb[:, :], mask_qk[:, :],
                                             start=False, stop=True)
                            at += n
                        last.then_inc(s_done, 1)

                def transpose_maxima(c):
                    out = free("M", c)
                    wait_apart(pe, apart["pe"], m_ready, rounds(b, NQ, c + 1))
                    pe.transpose(out[0:2 * 4 * TT, 0:P // 2].bitcast(BF16),
                                 mparts[:, :, :].rearrange("p a n -> p (a n)"), identb[:, :]).then_inc(tile_done, 1)

                def shifted_scores(h):
                    c, s = h // 4, h // 4 % SLOTS
                    if h == 0:
                        pe.wait_ge(act_read, rounds(b, ACT_READS, act_reads(PROLOGUE - 1)))
                        pe.wait_ge(dve_read, rounds(b, DVE_READS, dve_reads(PROLOGUE - 1)))
                    if h % 4 == 0:
                        pe.wait_ge(m_placed[c % 2], rounds(b, NQ // 2 * 32, (c // 2 + 1) * 32))
                    for k, tiles in enumerate(((0,), (1, 3), (2,))):
                        pe.wait_ge(exp_done, rounds(b, UNITS, 3 * h + k - 2))
                        at = 0
                        for t in tiles:
                            n = S - t * P
                            pe.matmul(bank[3 + k][:, at:at + n], k_st[0:K_EXP, s, h % 4, t * P:(t + 1) * P],
                                      q_st[0:K_EXP, s, h % 4, t * P:S], start=True, stop=False)
                            last = pe.matmul(bank[3 + k][:, at:at + P], identb[:, :], mask_kq[:, :],
                                             start=False, stop=True)
                            at += n
                        last.then_inc(t_done, 1)

                def weigh_values(c):
                    pe.wait_ge(exp_done, rounds(b, UNITS, QU * (c + 1)))
                    pe.wait_ge(pv_copied, rounds(b, NQ, c))
                    for t, at in ((0, 0), (1, 4 * P), (2, 8 * P), (3, 7 * P)):
                        n = S - t * P
                        for j in range(4):
                            last = pe.matmul(bank[6][32 * j:32 * j + 32, t * P:S], v_nat[:, t, 4 * c + j, :],
                                             pt[:, (4 * c + j) % PT_RING, at:at + n], start=(t == 0), stop=(t == TT - 1))
                    last.then_inc(pv_done, 1)

                def project_out():
                    outs = [free("P", t) for t in range(TT)]
                    for k in range(G):
                        if k >= G - 2:
                            pe.wait_ge(attn_split, rounds(b, G, k + 1))
                        for t in range(TT):
                            rows = slice(t * P, (t + 1) * P)
                            last = exact_product(pe, outs[t], [(fT_hi[:, k, rows], fT_lo[:, k, rows], wproj_hi[:, k, :],
                                                                wproj_lo[:, k, :])], start=(k == 0), stop=(k == G - 1))
                            if k == G - 1:
                                last.then_inc(tile_done, 1)

                transpose_tokens()
                for g in range(2):
                    project(0, g)
                    project(1, g)
                values(0)
                values(1)
                for h in range(4):
                    scores(h)
                values(2)
                values(3)
                transpose_maxima(0)
                for h in range(4, 8):
                    scores(h)
                for c in range(NQ):
                    for i in range(4):
                        shifted_scores(4 * c + i)
                        if c + 2 < NQ:
                            scores(4 * (c + 2) + i)
                        if i == 0 and c + 1 < NQ:
                            transpose_maxima(c + 1)
                        if i == 1 and c >= 1:
                            weigh_values(c - 1)
                        if i == 1 and c in (0, 2):
                            project(0, 2 + c // 2)
                        if i == 3 and c in (0, 2):
                            project(1, 2 + c // 2)
                weigh_values(NQ - 1)
                project_out()


def qkv_split_count():
    return 1 + KT - 1


def exact_product(pe, out, operands, start=True, stop=True):
    passes = [p for a_hi, a_lo, b_hi, b_lo in operands for p in ((a_hi, b_hi), (a_hi, b_lo), (a_lo, b_hi))]
    for i, (a, c) in enumerate(passes):
        last = pe.matmul(out[:, :], a, c, start=(start and i == 0), stop=(stop and i == len(passes) - 1))
    return last


def ffn(nc, x1_dram, wgu_d, wd_d, out_d, bank, ident, minus_half):
    out_v = out_d.rearrange("b (t p) d -> b t p d", p=P)
    RAW = 2

    with ExitStack() as ctx:
        def sb(name, shape, dt=F32):
            return ctx.enter_context(nc.sbuf_tensor(name, shape, dt))

        def sem(name):
            return ctx.enter_context(nc.semaphore(name))

        wgu_hi = sb("wgu_hi", [P, FT, 2, KT, P], F32R)
        wgu_lo = sb("wgu_lo", [P, FT, 2, KT, P], F32R)
        wd_hi = sb("wd_hi", [P, FT, D], F32R)
        wd_lo = sb("wd_lo", [P, FT, D], F32R)
        wgu_raw = sb("wgu_raw", [P, RAW, 2, KT, P])
        wd_raw = sb("wd_raw", [P, RAW, D])
        x1 = sb("x1", [P, TT, D])
        hn = sb("hn", [P, TT, D])
        stats = sb("stats2", [P, TT, 6])
        mv = sb("mv2", [P, TT, 2])
        rstd = sb("rstd2", [P, TT])
        hT_hi = sb("hT_hi", [P, KT, S], F32R)
        hT_lo = sb("hT_lo", [P, KT, S], F32R)
        silu = sb("silu", [P, 2, S])
        gu = sb("gu", [P, 2, S])
        gu_hi = sb("gu_hi", [P, 2, S], F32R)
        gu_lo = sb("gu_lo", [P, 2, S], F32R)

        w_in = [sem(f"w_in{s}") for s in range(RAW)]
        w_hi_done = sem("w_hi_done2")
        w_lo_done = sem("w_lo_done2")
        x1_in = sem("x1_in")
        step_done = sem("step_done2")
        apart = {e: sem(f"apart2_{e}") for e in ("pool", "dve")}
        moments_ready = sem("moments_ready2")
        var_ready = sem("var_ready2")
        rstd_ready = sem("rstd_ready2")
        normed = sem("normed2")
        t_done = sem("t_done2")
        hi_done = sem("hi_done")
        lo_done = sem("lo_done")
        gate_done = sem("gate_done")
        up_done = sem("up_done")
        silu_done = sem("silu_done")
        gu_done = sem("gu_done")
        gu_hi_done = sem("gu_hi_done")
        gu_lo_done = sem("gu_lo_done")
        down_done = sem("down_done")
        out_ready = sem("out_ready")
        out_stored = sem("out_stored")
        block = ctx.enter_context(nc.Block())
        FSTEPS = 1

        @block.sync
        def _(sp):
            for f in range(FT):
                if f >= RAW:
                    sp.wait_ge(w_lo_done, f - RAW + 1)
                sp.dma_start(wgu_raw[:, f % RAW, :, :, :], wgu_d[f]).then_inc(w_in[f % RAW], 16)
                sp.dma_start(wd_raw[:, f % RAW, :], wd_d[f]).then_inc(w_in[f % RAW], 16)

        @block.gpsimd
        def _(pool):
            with pool.Fori(0, B) as b:
                for t in range(TT):
                    pool.dma_start(x1[:, t, :], x1_dram[b, t]).then_inc(x1_in, 16)
                inverse_deviation(pool, apart["pool"], mv, rstd, minus_half, moments_ready, var_ready, rstd_ready, b + 1)
                for t in range(TT):
                    wait_apart(pool, apart["pool"], out_ready, rounds(b, TT, t + 1))
                    pool.dma_start(out_v[b, t], x1[:, t, :]).then_inc(out_stored, 16)
                wait_apart(pool, apart["pool"], out_stored, (b + 1) * 16 * TT)

        @block.scalar
        def _(act):
            for s, n in ((hi_done, KT), (silu_done, FT), (gu_hi_done, FT)):
                act.sem_inc(s, n)

            def weight_hi(f):
                act.wait_ge(w_in[f % RAW], 32 * (f // RAW + 1))
                act.copy(wgu_hi[:, f, :, :, :], wgu_raw[:, f % RAW, :, :, :])
                act.copy(wd_hi[:, f, :], wd_raw[:, f % RAW, :]).then_inc(w_hi_done, 1)

            for f in range(FT):
                weight_hi(f)
            with act.Fori(0, B) as b:
                for k in range(KT):
                    act.wait_ge(t_done, rounds(b, KT, k + 1))
                    act.copy(hT_hi[:, k, :], bank[4 + k][:, :]).then_inc(hi_done, 1)

                def gate(f):
                    act.wait_ge(gate_done, rounds(b, FT, f + 1))
                    act.wait_ge(gu_done, rounds(b, FT, f - 1))
                    act.activation(silu[:, f % 2, :], bank[4 + 2 * (f % 2)][:, :], ACT.Silu).then_inc(silu_done, 1)

                def high(f):
                    act.wait_ge(gu_done, rounds(b, FT, f + 1))
                    act.wait_ge(down_done, rounds(b, FT, f - 1))
                    act.copy(gu_hi[:, f % 2, :], gu[:, f % 2, :]).then_inc(gu_hi_done, 1)

                gate(0)
                for f in range(1, FT):
                    high(f - 1)
                    gate(f)
                high(FT - 1)

        @block.vector
        def _(dve):
            for s, n in ((step_done, FSTEPS), (normed, 1), (lo_done, KT), (gu_done, FT), (gu_lo_done, FT), (out_ready, TT)):
                dve.sem_inc(s, n)
            for f in range(FT):
                dve.wait_ge(w_hi_done, f + 1)
                dve.tensor_tensor(wgu_lo[:, f, :, :, :].rearrange("p c k n -> p (c k n)"),
                                  wgu_raw[:, f % RAW, :, :, :].rearrange("p c k n -> p (c k n)"),
                                  wgu_hi[:, f, :, :, :].rearrange("p c k n -> p (c k n)").bitcast(F32), ALU.subtract)
                dve.tensor_tensor(wd_lo[:, f, :], wd_raw[:, f % RAW, :], wd_hi[:, f, :].bitcast(F32),
                                  ALU.subtract).then_inc(w_lo_done, 1)
            with dve.Fori(0, B) as b:
                steps = [0]

                def step(ins):
                    steps[0] += 1
                    ins.then_inc(step_done, 1)
                    wait_apart(dve, apart["dve"], step_done, rounds(b, FSTEPS, steps[0]))

                dve.wait_ge(x1_in, (b + 1) * 16 * TT)
                layernorm(dve, step, x1, hn, stats, mv, rstd, moments_ready, rstd_ready, b + 1).then_inc(normed, 1)
                for k in range(KT):
                    dve.wait_ge(hi_done, rounds(b, KT, k + 1))
                    dve.tensor_tensor(hT_lo[:, k, :], bank[4 + k][:, :], hT_hi[:, k, :].bitcast(F32),
                                      ALU.subtract).then_inc(lo_done, 1)
                for f in range(FT):
                    dve.wait_ge(silu_done, rounds(b, FT, f + 1))
                    dve.wait_ge(up_done, rounds(b, FT, f + 1))
                    dve.wait_ge(gu_hi_done, rounds(b, FT, f - 1))
                    dve.tensor_tensor(gu[:, f % 2, :], bank[5 + 2 * (f % 2)][:, :], silu[:, f % 2, :],
                                      ALU.mult).then_inc(gu_done, 1)
                    dve.wait_ge(gu_hi_done, rounds(b, FT, f + 1))
                    dve.tensor_tensor(gu_lo[:, f % 2, :], gu[:, f % 2, :], gu_hi[:, f % 2, :].bitcast(F32),
                                      ALU.subtract).then_inc(gu_lo_done, 1)
                dve.wait_ge(down_done, rounds(b, FT, FT))
                for t in range(TT):
                    dve.tensor_tensor(x1[:, t, :], bank[t][:, :], x1[:, t, :], ALU.add).then_inc(out_ready, 1)
                assert steps[0] == FSTEPS

        @block.tensor
        def _(pe):
            for s, n in ((t_done, KT), (gate_done, FT), (up_done, FT), (down_done, FT)):
                pe.sem_inc(s, n)
            with pe.Fori(0, B) as b:
                pe.wait_ge(normed, rounds(b, 1, 1))
                pe.wait_ge(gu_done, rounds(b - 1, FT, FT))
                for k in range(KT):
                    for t in range(TT):
                        last = pe.transpose(bank[4 + k][:, t * P:(t + 1) * P], hn[:, t, k * P:(k + 1) * P], ident[:, :])
                    last.then_inc(t_done, 1)

                def gate_up(f):
                    if f < 2:
                        pe.wait_ge(lo_done, rounds(b, KT, KT))
                    pe.wait_ge(w_lo_done, f + 1)
                    for c, done in enumerate((gate_done, up_done)):
                        pe.wait_ge(gu_done, rounds(b, FT, f - 1))
                        exact_product(pe, bank[4 + 2 * (f % 2) + c],
                                      [(wgu_hi[:, f, c, k, :], wgu_lo[:, f, c, k, :], hT_hi[:, k, :], hT_lo[:, k, :])
                                       for k in range(KT)]).then_inc(done, 1)

                def down(f):
                    if f == 0:
                        pe.wait_ge(out_ready, rounds(b - 1, TT, TT))
                    pe.wait_ge(gu_lo_done, rounds(b, FT, f + 1))
                    for t in range(TT):
                        cols = slice(t * P, (t + 1) * P)
                        for i, (a, w) in enumerate(((gu_hi, wd_hi), (gu_hi, wd_lo), (gu_lo, wd_hi))):
                            last = pe.matmul(bank[t][:, :], a[:, f % 2, cols], w[:, f, :],
                                             start=(f == 0 and i == 0), stop=(f == FT - 1 and i == 2))
                    last.then_inc(down_done, 1)

                gate_up(0)
                for f in range(1, FT):
                    gate_up(f)
                    down(f - 1)
                down(FT - 1)


def kernel(**inputs):
    from concourse import bacc
    from concourse.bass_utils import run_bass_kernel_spmd

    def given(name):
        return np.ascontiguousarray(inputs["L0_" + name])

    def padded(w):
        return np.concatenate([w, np.zeros((FT * P - F, D), w.dtype)])

    both = np.stack([padded(given("ffn_w_gate")), padded(given("ffn_w_up"))])
    wgu = np.ascontiguousarray(both.reshape(2, FT, P, KT, P).transpose(1, 4, 0, 3, 2))
    wd = np.ascontiguousarray(padded(given("ffn_w_down").T).reshape(FT, P, D))
    q_rows, k_rows = extra_rows()

    def stacked_order(w):
        qk = w[..., :2 * D].reshape(*w.shape[:-1], 2 * G, HG, HD).swapaxes(-1, -2).reshape(*w.shape[:-1], 2 * D)
        return np.ascontiguousarray(np.concatenate([qk, w[..., 2 * D:]], -1))

    arrays = {
        "x": given("attn_hidden_states"), "w_qkv": stacked_order(given("attn_w_attn")),
        "b_qkv": stacked_order(given("attn_b_attn")),
        "w_proj": given("attn_w_proj"), "b_proj": given("attn_b_proj"), "w_gate_up": wgu, "w_down": wd,
        "q_rows": q_rows, "k_rows": k_rows,
    }
    nc = bacc.Bacc("TRN2", target_bir_lowering=False, num_devices=1)
    args = [nc.dram_tensor(n, a.shape, mybir.dt.from_np(a.dtype), kind="ExternalInput").ap() for n, a in arrays.items()]
    out = nc.dram_tensor("out", (B, S, D), F32, kind="ExternalOutput").ap()
    kernel_body(nc, *args, out)
    return run_bass_kernel_spmd(nc, [arrays], core_ids=[0]).results[0]["out"]
```

```python
from contextlib import ExitStack

import numpy as np

import concourse.bass as bass
from concourse import mybir

F32 = mybir.dt.float32
F32R = mybir.dt.float32r
BF16 = mybir.dt.bfloat16
ACT = mybir.ActivationFunctionType
ALU = mybir.AluOpType
AX = mybir.AxisListType

P = 128
B, S, D = 4, 512, 512
H, HD = 32, 16
F = 1376
KT = D // P
TT = S // P
HG = P // HD
G = H // HG
NQ = H // 4
QG = NQ // G
SLOTS = 4
FT = (F + P - 1) // P
EPS = 1e-5
NEG = -1e30

Q_TERM = (0, 1, 2, 0, 1, 0)
K_TERM = (0, 0, 0, 1, 1, 2)
TERMS = len(Q_TERM)
ROW_X = TERMS * HD
K_MAX = ROW_X + 1
K_EXP = ROW_X + 5

T_TILES, S_TILES = ((0,), (1, 3), (2,)), ((3,), (2,), (0, 1))
WIDE = (512, 512, 256)
COL0 = (0, 512, 1024)
NBLK = sum(WIDE) // P
BM_AT, BM_N = (12, 8, 3), (4, 3, 3)
PT_RING = 6

TILES = ([("V", 0), ("V", 1), ("Q", 1), ("K", 1), ("V", 2), ("M", 0), ("V", 3), ("M", 1), ("Q", 2), ("K", 2)]
         + [("M", 2), ("Q", 3), ("M", 3), ("K", 3)] + [("M", c) for c in range(4, NQ)]
         + [("T", k) for k in range(KT)] + [("Q", 0), ("K", 0)] + [("P", t) for t in range(TT)])
NT = len(TILES)
TILE_AT = {t: n for n, t in enumerate(TILES)}
BANKS = {"V": (3, 4, 4, 5), "Q": (0, 5, 6, 7), "K": (1, 3, 7, 7), "M": (7,) * NQ, "T": (0, 1, 2, 7), "P": (3, 4, 5, 7)}
TILE_BANK = [BANKS[kind][i] for kind, i in TILES]
BY_ACT = "TQKV"
BY_DVE = "TQKMP"


def act_reads(n):
    return sum(kind in BY_ACT for kind, _ in TILES[:n + 1])


def dve_reads(n):
    return sum(kind in BY_DVE for kind, _ in TILES[:n + 1])


def before_in_bank(n):
    earlier = [m for m in range(n) if TILE_BANK[m] == TILE_BANK[n]]
    return (0, earlier[-1]) if earlier else (1, max(m for m in range(NT) if TILE_BANK[m] == TILE_BANK[n]))


BETWEEN = {0: (0, 2, (0, 1)), 1: (0, 2, (2, 3)), 2: (1, 2, (0, 1)), 3: (1, 2, (2, 3)),
           6: (0, 3, (0, 1)), 7: (0, 3, (2, 3)), 10: (1, 3, (0, 1)), 11: (1, 3, (2, 3))}
COMPACT = 2


def made_in(b, g):
    return (b - 1, G - 1) if g == 0 else (b, g - 1)


ACT_READS, DVE_READS = act_reads(NT - 1), dve_reads(NT - 1)
XR_INCS = TT * 16
STEPS = 2 * NQ + 4


def slopes():
    start = 2.0 ** (-(2.0 ** -(np.log2(H) - 3)))
    return (start ** np.arange(1, H + 1, dtype=np.float32)).astype(np.float32)


def bf16_part(x):
    return (x.view(np.uint32) & np.uint32(0xFFFF0000)).view(np.float32)


def extra_rows():
    s, parts = slopes() * np.float32(HD), []
    for _ in range(3):
        p = bf16_part(s)
        parts.append(np.repeat(p[:, None], S, 1))
        s = s - p
    pos = np.arange(S, dtype=np.float32) - S // 2
    one = np.ones(S, np.float32)
    return np.concatenate(parts), np.stack([pos, one, pos, one, pos])


def rounds(b, per, k=0):
    return (b + 1) * per + k


def wait_apart(eng, apart, semaphore, value):
    eng.wait_ge(semaphore, value)
    eng.sem_inc(apart, 1)


def statistics(dve, src, stats, t):
    return dve.bn_stats(stats[:, t, :], src[:, t, :])


def moments(dve, stats, mv, moments_ready):
    for t in range(TT):
        last = dve.bn_aggr(mv[:, t, :], stats[:, t, :])
    last.then_inc(moments_ready, 1)


def normalise(dve, src, dst, mv, rstd, moments_ready, rstd_ready, count):
    dve.wait_ge(moments_ready, count)
    dve.wait_ge(rstd_ready, count)
    for t in range(TT):
        last = dve.tensor_scalar(dst[:, t, :], src[:, t, :], mv[:, t, 0:1], rstd[:, t:t + 1], ALU.subtract, ALU.mult)
    return last


def inverse_deviation(pool, apart, mv, rstd, minus_half, moments_ready, var_ready, rstd_ready, count):
    wait_apart(pool, apart, moments_ready, count)
    pool.tensor_scalar(mv[:, :, 1], mv[:, :, 1], EPS, None, ALU.add).then_inc(var_ready, 1)
    pool.wait_ge(var_ready, count)
    pool.tensor_tensor(rstd[:, :], mv[:, :, 1], minus_half[:, :], ALU.pow).then_inc(rstd_ready, 1)


def kernel_body(nc, x_d, wqkv_d, bqkv_d, wproj_d, bproj_d, wgu_d, wd_d, qx_d, kx_d, out_d):
    with ExitStack() as whole:
        bank = [whole.enter_context(nc.psum_tensor(f"bank{i}", [P, 512], F32)) for i in range(8)]
        ident = whole.enter_context(nc.sbuf_tensor("ident", [P, P], F32))
        minus_half = whole.enter_context(nc.sbuf_tensor("minus_half", [P, TT], F32))
        fT_hi = whole.enter_context(nc.sbuf_tensor("fT_hi", [P, KT, S], F32R))
        fT_lo = whole.enter_context(nc.sbuf_tensor("fT_lo", [P, KT, S], F32R))
        wgu_first = whole.enter_context(nc.sbuf_tensor("wgu_first", [P, 2, KT, P], F32))
        first_in = whole.enter_context(nc.semaphore("first_in"))
        x1_stored = whole.enter_context(nc.semaphore("x1_stored"))
        tokens_dram = nc.dram_tensor("tokens_dram", [2 * B, TT, P, D], F32, kind="Internal").ap()
        attention(nc, x_d, wqkv_d, bqkv_d, wproj_d, bproj_d, qx_d, kx_d, tokens_dram, bank, ident, minus_half, fT_hi, fT_lo,
                  wgu_d, wgu_first, first_in, x1_stored)
        ffn(nc, tokens_dram, wgu_d, wd_d, out_d, bank, ident, minus_half, fT_hi, fT_lo, wgu_first, first_in,
            x1_stored)


def attention(nc, x_d, wqkv_d, bqkv_d, wproj_d, bproj_d, qx_d, kx_d, tokens_dram, bank, ident, minus_half, fT_hi, fT_lo,
              wgu_d, wgu_first, first_in, x1_stored):
    x_v = x_d.rearrange("b (t p) d -> b t p d", p=P)
    stack_dram = nc.dram_tensor("stack_dram", [2, G, TERMS, P, S], BF16, kind="Internal").ap()
    slopes_dram = nc.dram_tensor("slopes_dram", [3, H, S], BF16, kind="Internal").ap()
    k_rows_dram = nc.dram_tensor("k_rows_dram", [K_EXP - ROW_X, S], BF16, kind="Internal").ap()
    inv_dram = nc.dram_tensor("inv_dram", [COMPACT, HG, S], F32, kind="Internal").ap()
    pv_dram = nc.dram_tensor("pv_dram", [G, QG * P, S], F32, kind="Internal").ap()

    with ExitStack() as ctx:
        def sb(name, shape, dt=F32):
            return ctx.enter_context(nc.sbuf_tensor(name, shape, dt))

        def sem(name):
            return ctx.enter_context(nc.semaphore(name))

        wqkv_hi = sb("wqkv_hi", [P, KT, 3 * D], F32R)
        wqkv_lo = sb("wqkv_lo", [P, KT, 3 * D], F32R)
        wproj_hi = sb("wproj_hi", [P, KT, D], F32R)
        wproj_lo = sb("wproj_lo", [P, KT, D], F32R)
        bias_qkv = sb("bias_qkv", [P, 3 * G])
        bproj = sb("bproj", [P, D])
        identb = sb("identb", [P, P], BF16)
        mask_qk = sb("mask_qk", [P, P], BF16)
        mask_kq = sb("mask_kq", [P, P], BF16)
        xt = sb("xt", [P, TT, D])
        stats = sb("stats", [P, TT, 6])
        mv = sb("mv", [P, TT, 2])
        rstd = sb("rstd", [P, TT])
        aT_hi = sb("aT_hi", [P, G, S], F32R)
        aT_lo = sb("aT_lo", [P, G, S], F32R)
        part = sb("part", [P, 2, 3, S], BF16)
        rest = sb("rest", [P, S])
        q_st = sb("q_st", [P, SLOTS, 4, S], BF16)
        k_st = sb("k_st", [P, SLOTS, 4, S], BF16)
        pt = sb("pt", [P, PT_RING, NBLK * P])
        v_nat = sb("v_nat", [P, TT, H, 2 * HD])
        bm = sb("bm", [P, 4, TT * TT])
        mx = sb("mx", [P, 4, TT])
        mparts = sb("mparts", [P, 2, 4 * TT], BF16)
        mt = sb("mt", [2 * 4 * TT, 2, P], BF16)
        weighed = sb("weighed", [P, 4, S])
        pv_raw = weighed[:, 0:2, :]
        attnT = weighed[:, 2, :]
        sums = weighed[:, 3, :]
        XR_SLOTS = (2, 3)
        xr = pt[:, XR_SLOTS[0]:XR_SLOTS[-1] + 1, :].rearrange("p a b -> p (a b)")[:, 0:TT * D].rearrange("p (t d) -> p t d", t=TT)
        pt_flat, n = pt[:, :, :].rearrange("p a b -> p (a b)"), KT * 3 * D
        wqkv_raw = pt_flat[:, 0:n].rearrange("p (k n) -> p k n", k=KT)
        wproj_raw = weighed
        row_sums = sb("row_sums", [P, HG * S // P])
        qx_raw = pt_flat[0:3 * H, n:n + S]
        kx_raw = pt_flat[ROW_X:K_EXP, n + S:n + 2 * S]
        qx_sb = q_st[0:3 * H, SLOTS - 1, 0, :]
        kx_sb = q_st[ROW_X:K_EXP, SLOTS - 1, 1, :]

        rows_in = sem("rows_in")
        bias_in = sem("bias_in")
        wqk_in = [sem(f"wqk_in{k}") for k in range(KT)]
        wv_in = sem("wv_in")
        wproj_in = sem("wproj_in")
        bproj_in = sem("bproj_in")
        zeroed = sem("zeroed")
        masks_made = sem("masks_made")
        w_hi_done = sem("w_hi_done")
        w_split = sem("w_split")
        w_split_v = sem("w_split_v")
        rows_cast = sem("rows_cast")
        rows_stored = sem("rows_stored")
        k_rows_in = sem("k_rows_in")
        copied = sem("copied")
        x_in = [sem(f"x_in{t}") for t in range(TT)]
        apart = {e: sem(f"apart_{e}") for e in ("sp", "pool", "dve", "pe")}
        step_done = sem("step_done")
        moments_ready = sem("moments_ready")
        var_ready = sem("var_ready")
        rstd_ready = sem("rstd_ready")
        normed = sem("normed")
        tile_done = sem("tile_done")
        act_read = sem("act_read")
        dve_read = sem("dve_read")
        p2_done = sem("p2_done")
        p3_done = sem("p3_done")
        parts_stored = [sem("q_stored"), sem("k_stored")]
        stacked = [sem(f"stacked{s}") for s in range(SLOTS)]
        s_done = sem("s_done")
        s_maxed = sem("s_maxed")
        m_ready = sem("m_ready")
        m_placed = [sem(f"m_placed{i}") for i in range(2)]
        t_done = sem("t_done")
        exp_done = sem("exp_done")
        pv_done = sem("pv_done")
        pv_copied = sem("pv_copied")
        pv_stored = [sem(f"pv_stored{i}") for i in range(2)]
        row_sums_in = sem("row_sums_in")
        inverted = sem("inverted")
        inv_stored = sem("inv_stored")
        attn_in = sem("attn_in")
        attn_ready = sem("attn_ready")
        attn_hi = sem("attn_hi")
        attn_split = sem("attn_split")
        xr_in = sem("xr_in")
        xr_biased = sem("xr_biased")
        x1_ready = sem("x1_ready")
        block = ctx.enter_context(nc.Block())

        UNITS = 3 * H
        QU = 3 * 4
        STACK_INCS = 3 * 16
        HALVES = 2
        HS = S // HALVES
        PARTS_INCS = 3 * 16

        def stacked_count(b, c):
            return rounds(b - 1, 2 * STACK_INCS, 2 * STACK_INCS) if c < QG else rounds(
                b, 2 * STACK_INCS, (2 if c >= QG + SLOTS else 1) * STACK_INCS)

        @block.sync
        def _(sp):
            for t in range(TT):
                sp.dma_start(xt[:, t, :], x_v[0, t]).then_inc(x_in[t], 16)
            sp.dma_start(qx_raw, qx_d).then_inc(rows_in, 16)
            sp.dma_start(kx_raw, kx_d).then_inc(rows_in, 16)
            for k in range(KT):
                sp.dma_start(wqkv_raw[:, k, 0:2 * D], wqkv_d[k * P:(k + 1) * P, 0:2 * D]).then_inc(wqk_in[k], 16)
            with nc.allow_non_contiguous_dma(reason="biases, once, a column per partition"):
                sp.dma_start(bias_qkv[:, :], bqkv_d.rearrange("(c p) -> p c", p=P)).then_inc(bias_in, 16)
            sp.dma_start(wqkv_raw[:, :, 2 * D:3 * D],
                         wqkv_d.rearrange("(k p) n -> p k n", p=P)[:, :, 2 * D:3 * D]).then_inc(wv_in, 16)
            sp.dma_start(wproj_raw[:, :, :], wproj_d.rearrange("(k p) n -> p k n", p=P)).then_inc(wproj_in, 16)
            sp.dma_start(bproj[:, :], bproj_d.rearrange("(a d) -> a d", a=1).broadcast_to([P, D])).then_inc(bproj_in, 16)
            for s, n in ([(x, (G - 1) * PARTS_INCS) for x in parts_stored] + [(x, NQ // 2 * 32) for x in m_placed]
                         + [(stacked[s], (1 if s < QG else 2) * STACK_INCS) for s in range(SLOTS)]
                         + [(x, NQ // 2 * 16) for x in pv_stored]
                         + [(row_sums_in, COMPACT * 16), (inv_stored, COMPACT * 16), (attn_in, G * 32),
                            (xr_in, XR_INCS), (x1_stored, XR_INCS)]):
                sp.sem_inc(s, n)
            sp.wait_ge(rows_cast, 2)
            sp.dma_start(slopes_dram.rearrange("a h s -> (a h) s"), qx_sb).then_inc(rows_stored, 16)
            sp.dma_start(k_rows_dram, kx_sb).then_inc(rows_stored, 16)
            sp.wait_ge(rows_stored, 32)
            sp.dma_start(k_st[ROW_X:K_EXP, :, :, :].rearrange("p a h s -> p (a h) s"),
                         k_rows_dram.rearrange("p (a s) -> p a s", a=1).broadcast_to([K_EXP - ROW_X, SLOTS * 4, S])
                         ).then_inc(k_rows_in, 16)

            def store_parts(b, g):
                b, n = made_in(b, g)
                q_parts, k_parts = part[:, 0, :, :], part[:, 1, :, :]
                sources = ((q_parts[:, 0:3, :], q_parts[:, 0:2, :], q_parts[:, 0:1, :]),
                           [k_parts[:, i:i + 1, :].broadcast_to([P, m, S]) for i, m in enumerate((3, 2, 1))])
                for c in range(2):
                    sp.wait_ge(p3_done, rounds(b, 2 * G, 2 * n + c + 1))
                    for r, m, src in zip((0, 3, 5), (3, 2, 1), sources[c]):
                        sp.dma_start(stack_dram[c, g, r:r + m].rearrange("r p s -> p r s"), src).then_inc(parts_stored[c], 16)

            def load_stacks(b, c):
                g, at, s = c // QG, c % QG * 4, c % SLOTS
                wait_apart(sp, apart["sp"], t_done, rounds(b, UNITS, QU * (c + 1 - SLOTS)))
                made, n = made_in(b, g)
                for i, st in enumerate((q_st, k_st)):
                    sp.wait_ge(parts_stored[i], rounds(made, G * PARTS_INCS, (n + 1) * PARTS_INCS))
                    sp.dma_start(st[0:ROW_X, s, :, :], stack_dram[i, g].rearrange("r (e h) s -> (r e) h s", h=HG)
                                 [:, at:at + 4, :]).then_inc(stacked[s], 16)
                sp.dma_start(q_st[ROW_X:K_EXP:2, s, :, :], slopes_dram[:, 4 * c:4 * c + 4, :]).then_inc(stacked[s], 16)

            store_parts(0, 0)
            for c in range(QG):
                load_stacks(0, c)
            sp.dma_start(wgu_first[:, :, :, :], wgu_d[0]).then_inc(first_in, 16)
            sp.dma_start(tokens_dram[1].rearrange("t p d -> (t p) d"), x_d[1]).then_inc(copied, 16)
            with sp.Fori(0, B) as b:
                def load_next_tokens():
                    wait_apart(sp, apart["sp"], tile_done, rounds(b - 1, NT, TILE_AT["T", KT - 1] + 1))
                    wait_apart(sp, apart["sp"], copied, (b + 1) * 16)
                    wait_apart(sp, apart["sp"], x1_stored, rounds(b, XR_INCS, 0))
                    for t in range(TT):
                        sp.dma_start(xt[:, t, :], tokens_dram[b + 1, t]).then_inc(x_in[t], 16)

                def store_pv(c):
                    sp.wait_ge(pv_copied, rounds(b, NQ, c + 1))
                    sp.dma_start(pv_dram[c // QG, c % QG * P:(c % QG + 1) * P, :], pv_raw[:, c % 2, :]).then_inc(pv_stored[c % 2], 16)

                def load_row_sums(g):
                    for i in range(2):
                        sp.wait_ge(pv_stored[i], rounds(b, G * 16, (g + 1) * 16))
                    sp.dma_start(row_sums[:, :], pv_dram[g].rearrange("(h e) (a s) -> h e a s", e=2 * HD, a=P // HG)
                                 [:, HD, :, :]).then_inc(row_sums_in, 16)

                def load_group(g):
                    rows = pv_dram[g].rearrange("(h e) s -> h e s", e=2 * HD)
                    sums_src = rows[:, HD:2 * HD, :]
                    if g < COMPACT:
                        wait_apart(sp, apart["sp"], inverted, rounds(b, COMPACT, g + 1))
                        sp.dma_start(inv_dram[g].rearrange("h (a s) -> h a s", a=P // HG), row_sums[:, :]).then_inc(inv_stored, 16)
                        wait_apart(sp, apart["sp"], inv_stored, rounds(b, COMPACT * 16, (g + 1) * 16))
                        sums_src = inv_dram[g].rearrange("h (o s) -> h o s", o=1).broadcast_to([HG, HD, S])
                    wait_apart(sp, apart["sp"], attn_split, rounds(b, G * HALVES, g * HALVES))
                    for i in range(2):
                        sp.wait_ge(pv_stored[i], rounds(b, G * 16, (g + 1) * 16))
                    sp.dma_start(sums[:, :], sums_src).then_inc(attn_in, 16)
                    sp.dma_start(attnT[:, :], rows[:, 0:HD, :]).then_inc(attn_in, 16)

                load_next_tokens()
                store_parts(b, 1)
                load_stacks(b, 2)
                load_stacks(b, 3)
                sp.dma_start(tokens_dram[(b + 2) % B].rearrange("t p d -> (t p) d"), x_d[(b + 2) % B]).then_inc(copied, 16)
                for c in range(1, NQ):
                    if c in (1, 3):
                        store_parts(b, 2 + c // 2)
                    if c + SLOTS - 1 < NQ:
                        load_stacks(b, c + SLOTS - 1)
                    if c == NQ - 1:
                        wait_apart(sp, apart["sp"], pv_done, rounds(b, NQ, NQ - 1))
                        for t in range(TT):
                            sp.dma_start(xr[:, t, :], x_v[b, t]).then_inc(xr_in, 16)
                    if c in (3, 5):
                        load_group((c - 3) // 2)
                    store_pv(c - 1)
                    if c in (2, 4):
                        load_row_sums(c // 2 - 1)
                    if c == 6:
                        load_group(2)
                store_pv(NQ - 1)
                load_group(G - 1)
                store_parts(b + 1, 0)
                for c in range(QG):
                    load_stacks(b + 1, c)
                for t in range(TT):
                    wait_apart(sp, apart["sp"], x1_ready, rounds(b, TT, t + 1))
                    sp.dma_start(tokens_dram[b + B, t], xr[:, t, :]).then_inc(x1_stored, 16)
            for s in parts_stored:
                sp.wait_ge(s, rounds(B - 1, G * PARTS_INCS, G * PARTS_INCS))
            for s in stacked:
                sp.wait_ge(s, rounds(B - 1, 2 * STACK_INCS, 2 * STACK_INCS))
            sp.wait_ge(copied, (B + 1) * 16)
            for t in range(TT):
                sp.wait_ge(x_in[t], 16 * (B + 1))

        @block.gpsimd
        def _(pool):
            for m in (ident, identb, mask_qk, mask_kq):
                pool.memset(m[:, :], 0.0).then_inc(zeroed, 1)
            pool.memset(minus_half[:, :], -0.5).then_inc(zeroed, 1)
            pool.memset(bm[:, :, :], NEG).then_inc(zeroed, 1)
            pool.memset(v_nat[:, :, :, HD:2 * HD], 1.0).then_inc(zeroed, 1)
            pool.wait_ge(zeroed, 7)
            for m in (ident, identb):
                pool.affine_select(out=m[:, :], in_=m[:, :], compare_op=ALU.not_equal, fill=1.0, base=0,
                                   pattern=[[-1, P]], channel_multiplier=1).then_inc(masks_made, 1)
            for m, sign in ((mask_qk, 1), (mask_kq, -1)):
                pool.affine_select(out=m[:, :], in_=m[:, :], compare_op=ALU.is_ge, fill=NEG, base=0,
                                   pattern=[[-sign, P]], channel_multiplier=sign).then_inc(masks_made, 1)
            for s, n in ((p3_done, 2 * G - 2), (xr_biased, 1)):
                pool.sem_inc(s, n)
            inverse_deviation(pool, apart["pool"], mv, rstd, minus_half, moments_ready, var_ready, rstd_ready, 1)
            for k in range(2):
                pool.wait_ge(w_hi_done, k + 1)
                pool.tensor_tensor(wqkv_lo[:, k, 0:2 * D], wqkv_raw[:, k, 0:2 * D], wqkv_hi[:, k, 0:2 * D].bitcast(F32),
                                   ALU.subtract).then_inc(w_split, 1)

            def third_parts(b, g):
                b, n = made_in(b, g)
                for c in range(2):
                    wait_apart(pool, apart["pool"], p2_done, rounds(b, 2 * G, 2 * n + c + 1))
                    pool.tensor_tensor(part[:, c, 2, :], rest[:, :], part[:, c, 1, :], ALU.subtract).then_inc(p3_done, 1)

            third_parts(0, 0)
            pool.wait_ge(bproj_in, 16)
            with pool.Fori(0, B) as b:
                for g in range(1, G):
                    third_parts(b, g)
                inverse_deviation(pool, apart["pool"], mv, rstd, minus_half, moments_ready, var_ready, rstd_ready, b + 2)
                wait_apart(pool, apart["pool"], xr_in, rounds(b, XR_INCS, XR_INCS))
                for t in range(TT):
                    last = pool.tensor_tensor(xr[:, t, :], xr[:, t, :], bproj[:, :], ALU.add)
                last.then_inc(xr_biased, 1)
                third_parts(b + 1, 0)

        @block.scalar
        def _(act):
            for s, n in ((act_read, ACT_READS - KT - 2), (exp_done, UNITS), (pv_copied, NQ), (p2_done, 2 * G - 2),
                         (attn_hi, G * HALVES)):
                act.sem_inc(s, n)
            for k in range(KT):
                act.wait_ge(wqk_in[k], 16)
                act.copy(wqkv_hi[:, k, 0:2 * D], wqkv_raw[:, k, 0:2 * D]).then_inc(w_hi_done, 1)

            def transposed_hi(b):
                for k in range(KT):
                    n = TILE_AT["T", k]
                    act.wait_ge(tile_done, rounds(b, NT, n + 1))
                    act.copy(fT_hi[:, k, :], bank[TILE_BANK[n]][:, :]).then_inc(act_read, 1)

            transposed_hi(-1)
            act.wait_ge(wv_in, 16)
            act.copy(wqkv_hi[:, :, 2 * D:3 * D], wqkv_raw[:, :, 2 * D:3 * D]).then_inc(w_hi_done, 1)
            act.wait_ge(bias_in, 16)

            def first_part(b, c, g):
                b, n = made_in(b, g)
                tile = TILE_AT["QK"[c], g]
                act.wait_ge(tile_done, rounds(b, NT, tile + 1))
                act.wait_ge(parts_stored[c], rounds(b, G * PARTS_INCS, n * PARTS_INCS))
                act.activation(part[:, c, 0, :], bank[TILE_BANK[tile]][:, :], ACT.Identity,
                               bias=bias_qkv[:, c * G + g:c * G + g + 1]).then_inc(act_read, 1)

            def second_part(b, c, g):
                b, n = made_in(b, g)
                act.wait_ge(dve_read, rounds(b, DVE_READS, dve_reads(TILE_AT["QK"[c], g])))
                act.copy(part[:, c, 1, :], rest[:, :]).then_inc(p2_done, 1)

            def parts_of(b, g):
                for c in range(2):
                    first_part(b, c, g)
                    second_part(b, c, g)

            parts_of(0, 0)
            act.wait_ge(wproj_in, 16)
            act.copy(wproj_hi[:, :, :], wproj_raw[:, :, :]).then_inc(w_hi_done, 1)
            with act.Fori(0, B) as b:
                def copy_values(t):
                    n = TILE_AT["V", t]
                    act.wait_ge(tile_done, rounds(b, NT, n + 1))
                    act.copy(v_nat[:, t, :, 0:HD],
                             bank[TILE_BANK[n]][:, :].rearrange("p (h e) -> p h e", e=HD)).then_inc(act_read, 1)

                def exponentials(h):
                    if h == 0:
                        act.wait_ge(w_split, 2)
                        act.wait_ge(rows_cast, 2)
                        act.wait_ge(w_split_v, v_split_count())
                    if h >= PT_RING:
                        act.wait_ge(pv_done, rounds(b, NQ, (h - PT_RING) // 4 + 1))
                    elif h in XR_SLOTS:
                        act.wait_ge(x1_stored, rounds(b, XR_INCS, 0))
                    for k in range(3):
                        act.wait_ge(t_done, rounds(b, UNITS, 3 * h + k + 1))
                        act.activation(pt[:, h % PT_RING, COL0[k]:COL0[k] + WIDE[k]], bank[3 + k][:, 0:WIDE[k]],
                                       ACT.Exp, scale=1.0 / HD).then_inc(exp_done, 1)

                def copy_pv(c):
                    if c == 0:
                        act.wait_ge(w_split_v, v_split_count() + 1)
                    act.wait_ge(pv_done, rounds(b, NQ, c + 1))
                    act.wait_ge(pv_stored[c % 2], rounds(b, G * 16, c // 2 * 16))
                    act.copy(pv_raw[:, c % 2, :], bank[6][:, :]).then_inc(pv_copied, 1)

                def attention_hi(g):
                    if g == 0:
                        act.wait_ge(tile_done, rounds(b, NT, 0))
                    for i in range(HALVES):
                        at = slice(i * HS, (i + 1) * HS)
                        act.wait_ge(attn_ready, rounds(b, G * HALVES, g * HALVES + i + 1))
                        act.activation(aT_hi[:, g, at], attnT[:, at], ACT.Identity,
                                       bias=bias_qkv[:, 2 * G + g:2 * G + g + 1]).then_inc(attn_hi, 1)

                def place_maxima(c):
                    n = 4 * TT
                    act.wait_ge(dve_read, rounds(b, DVE_READS, dve_reads(TILE_AT["M", c])))
                    for a in range(2):
                        row = ROW_X + 1 + 2 * a
                        act.dma_start(q_st[row:row + 1, c % SLOTS, :, :].rearrange("p h (t n) -> p (h t) n", n=P),
                                      mt[a * n:(a + 1) * n, c % 2, :]).then_inc(m_placed[c % 2], 16)

                copy_values(0)
                copy_values(1)
                parts_of(b, 1)
                copy_values(2)
                place_maxima(0)
                copy_values(3)
                for c in range(NQ):
                    exponentials(4 * c)
                    if 1 <= c <= 3:
                        second_part(b, c % 2, 2 + c // 2)
                    exponentials(4 * c + 1)
                    if c + 1 < NQ:
                        place_maxima(c + 1)
                    if c == 0:
                        first_part(b, 0, 2)
                    exponentials(4 * c + 2)
                    if c == 0:
                        second_part(b, 0, 2)
                    if c >= 1:
                        copy_pv(c - 1)
                    if c in (4, 6):
                        attention_hi(c // 2 - 2)
                    exponentials(4 * c + 3)
                    if c <= 2:
                        first_part(b, (c + 1) % 2, 2 + (c + 1) // 2)
                transposed_hi(b)
                copy_pv(NQ - 1)
                attention_hi(2)
                parts_of(b + 1, 0)
                attention_hi(G - 1)

        @block.vector
        def _(dve):
            for s, n in ((step_done, STEPS), (dve_read, DVE_READS - KT - 2 - TT), (s_maxed, UNITS), (m_ready, NQ),
                         (inverted, COMPACT), (attn_ready, G * HALVES), (attn_split, G * HALVES), (x1_ready, TT)):
                dve.sem_inc(s, n)
            first_steps = [0]

            def first_step(ins):
                first_steps[0] += 1
                ins.then_inc(w_split_v, 1)
                dve.wait_ge(w_split_v, first_steps[0])

            for t in range(TT):
                dve.wait_ge(x_in[t], 16)
                last = statistics(dve, xt, stats, t)
            first_step(last)
            moments(dve, stats, mv, moments_ready)
            normalise(dve, xt, xt, mv, rstd, moments_ready, rstd_ready, 1).then_inc(normed, 1)
            dve.wait_ge(rows_in, 32)
            dve.tensor_copy(qx_sb, qx_raw).then_inc(rows_cast, 1)
            dve.tensor_copy(kx_sb, kx_raw).then_inc(rows_cast, 1)
            for k in range(2, KT):
                dve.wait_ge(w_hi_done, k + 1)
                first_step(dve.tensor_tensor(wqkv_lo[:, k, 0:2 * D], wqkv_raw[:, k, 0:2 * D],
                                             wqkv_hi[:, k, 0:2 * D].bitcast(F32), ALU.subtract))
            assert first_steps[0] == qk_split_count()

            def transposed_lo(b):
                for k in range(KT):
                    n = TILE_AT["T", k]
                    dve.wait_ge(act_read, rounds(b, ACT_READS, act_reads(n)))
                    dve.tensor_tensor(fT_lo[:, k, :], bank[TILE_BANK[n]][:, :], fT_hi[:, k, :].bitcast(F32),
                                      ALU.subtract).then_inc(dve_read, 1)

            transposed_lo(-1)
            dve.wait_ge(bias_in, 16)
            dve.wait_ge(w_hi_done, KT + 1)
            first_step(dve.tensor_tensor(wqkv_lo[:, :, 2 * D:3 * D], wqkv_raw[:, :, 2 * D:3 * D],
                                         wqkv_hi[:, :, 2 * D:3 * D].bitcast(F32), ALU.subtract))
            assert first_steps[0] == v_split_count()

            def done(b, kind, i):
                n = TILE_AT[kind, i]
                dve.wait_ge(tile_done, rounds(b, NT, n + 1))
                if kind in BY_ACT:
                    dve.wait_ge(act_read, rounds(b, ACT_READS, act_reads(n)))
                return bank[TILE_BANK[n]]

            def remainder(b, c, g):
                b, n = made_in(b, g)
                src = done(b, "QK"[c], g)
                dve.wait_ge(p3_done, rounds(b, 2 * G, 2 * n + c))
                dve.scalar_tensor_tensor(out=rest[:, :], in0=src[:, :],
                                         scalar=bias_qkv[:, c * G + g:c * G + g + 1], in1=part[:, c, 0, :],
                                         op0=ALU.add, op1=ALU.subtract).then_inc(dve_read, 1)

            remainder(0, 0, 0)
            remainder(0, 1, 0)
            dve.wait_ge(dve_read, DVE_READS - TT)
            dve.sem_inc(dve_read, TT)
            dve.wait_ge(w_hi_done, KT + 2)
            first_step(dve.tensor_tensor(wproj_lo[:, :, :], wproj_raw[:, :, :], wproj_hi[:, :, :].bitcast(F32), ALU.subtract))
            with dve.Fori(0, B) as b:
                steps = [0]

                def step(ins):
                    steps[0] += 1
                    ins.then_inc(step_done, 1)
                    wait_apart(dve, apart["dve"], step_done, rounds(b, STEPS, steps[0]))

                def block_maxima(h):
                    for k in range(3):
                        dve.wait_ge(s_done, rounds(b, UNITS, 3 * h + k + 1))
                        dve.tensor_reduce(bm[:, h % 4, BM_AT[k]:BM_AT[k] + BM_N[k]],
                                          bank[k][:, 0:BM_N[k] * P].rearrange("p (n q) -> p n q", q=P), AX.X,
                                          ALU.max).then_inc(s_maxed, 1)

                def row_maxima(c):
                    dve.wait_ge(s_maxed, rounds(b, UNITS, QU * (c + 1)))
                    step(dve.tensor_reduce(mx[:, :, :], bm[:, :, :].rearrange("p h (t n) -> p (h t) n", n=TT), AX.X, ALU.max))
                    flat = mx[:, :, :].rearrange("p h t -> p (h t)")
                    step(dve.tensor_scalar(mparts[:, 0, :], flat, -1.0, None, ALU.mult))
                    dve.scalar_tensor_tensor(out=mparts[:, 1, :], in0=flat, scalar=-1.0, in1=mparts[:, 0, :],
                                             op0=ALU.mult, op1=ALU.subtract).then_inc(m_ready, 1)

                def copy_maxima(c):
                    src = done(b, "M", c)
                    dve.wait_ge(m_placed[c % 2], rounds(b, NQ // 2 * 32, c // 2 * 32))
                    dve.tensor_copy(mt[:, c % 2, :], src[0:2 * 4 * TT, 0:P // 2].bitcast(BF16)).then_inc(dve_read, 1)

                def invert_sums(g, q):
                    dve.wait_ge(attn_in, rounds(b, G * 32, (g + 1) * 32))
                    return dve.reciprocal(sums[:, q * P:(q + 1) * P], sums[:, q * P:(q + 1) * P])

                def divide(g, halves=range(HALVES)):
                    if g < COMPACT:
                        dve.wait_ge(attn_in, rounds(b, G * 32, (g + 1) * 32))
                    for i in halves:
                        at = slice(i * HS, (i + 1) * HS)
                        dve.tensor_tensor(attnT[:, at], attnT[:, at], sums[:, at], ALU.mult).then_inc(attn_ready, 1)

                def attention_lo(g, halves=range(HALVES)):
                    if g == 0:
                        dve.wait_ge(tile_done, rounds(b, NT, 0))
                    for i in halves:
                        at = slice(i * HS, (i + 1) * HS)
                        dve.wait_ge(attn_hi, rounds(b, G * HALVES, g * HALVES + i + 1))
                        dve.scalar_tensor_tensor(out=aT_lo[:, g, at], in0=attnT[:, at],
                                                 scalar=bias_qkv[:, 2 * G + g:2 * G + g + 1],
                                                 in1=aT_hi[:, g, at].bitcast(F32),
                                                 op0=ALU.add, op1=ALU.subtract).then_inc(attn_split, 1)

                def invert_row_sums(g):
                    dve.wait_ge(row_sums_in, rounds(b, COMPACT * 16, (g + 1) * 16))
                    dve.reciprocal(row_sums[:, :], row_sums[:, :]).then_inc(inverted, 1)

                for h in range(8):
                    block_maxima(h)
                    if h == 1:
                        remainder(b, 0, 1)
                    if h % 4 == 3:
                        row_maxima(h // 4)
                    if h == 3:
                        remainder(b, 1, 1)
                    if h == 5:
                        copy_maxima(0)
                for c in range(NQ):
                    for i in range(4):
                        if c + 2 < NQ:
                            block_maxima(4 * (c + 2) + i)
                        if i == 1 and c + 1 < NQ:
                            copy_maxima(c + 1)
                        if (c, i) == (0, 1):
                            remainder(b, 0, 2)
                        if i == 3 and c <= 2:
                            remainder(b, (c + 1) % 2, 2 + (c + 1) // 2)
                        if (c, i) == (4, 1):
                            divide(0)
                        if (c, i) == (4, 3):
                            attention_lo(0)
                        if i == 1 and c in (3, 5):
                            invert_row_sums((c - 3) // 2)
                        if i in (0, 2) and c in (1, 2):
                            t = 2 * (c - 1) + i // 2
                            dve.wait_ge(x_in[t], (b + 2) * 16)
                            last = statistics(dve, xt, stats, t)
                            if t == TT - 1:
                                step(last)
                    if c + 2 < NQ:
                        row_maxima(c + 2)
                    if c == 3:
                        moments(dve, stats, mv, moments_ready)
                    if c == NQ - 2:
                        divide(1)
                        normalise(dve, xt, xt, mv, rstd, moments_ready, rstd_ready, b + 2).then_inc(normed, 1)
                        attention_lo(1)
                    if c == NQ - 1:
                        for q in range(4):
                            last = invert_sums(2, q)
                        step(last)
                transposed_lo(b)
                divide(2)
                attention_lo(2)
                remainder(b + 1, 0, 0)
                remainder(b + 1, 1, 0)
                invert_sums(3, 0)
                step(invert_sums(3, 1))
                divide(3, (0,))
                invert_sums(3, 2)
                attention_lo(3, (0,))
                step(invert_sums(3, 3))
                divide(3, (1,))
                attention_lo(3, (1,))
                dve.wait_ge(xr_biased, rounds(b, 1, 1))
                for t in range(TT):
                    dve.tensor_tensor(xr[:, t, :], done(b, "P", t)[:, :], xr[:, t, :], ALU.add).then_inc(dve_read, 1)
                    dve.wait_ge(dve_read, rounds(b, DVE_READS, dve_reads(TILE_AT["P", t])))
                    dve.sem_inc(x1_ready, 1)
                assert steps[0] == STEPS, (steps[0], STEPS)

        @block.tensor
        def _(pe):
            for s, n in ((tile_done, TILE_AT["T", 0]), (s_done, UNITS), (t_done, UNITS), (pv_done, NQ)):
                pe.sem_inc(s, n)
            pe.wait_ge(masks_made, 4)

            def transpose_tokens(b):
                pe.wait_ge(normed, b + 2)
                for k in range(KT):
                    n = TILE_AT["T", k]
                    for t in range(TT):
                        last = pe.transpose(bank[TILE_BANK[n]][:, t * P:(t + 1) * P], xt[:, t, k * P:(k + 1) * P], ident[:, :])
                    last.then_inc(tile_done, 1)

            def free(b, kind, i):
                n = TILE_AT[kind, i]
                back, m = before_in_bank(n)
                pe.wait_ge(act_read, rounds(b - back, ACT_READS, act_reads(m)))
                pe.wait_ge(dve_read, rounds(b - back, DVE_READS, dve_reads(m)))
                return bank[TILE_BANK[n]]

            def project(b, c, g, parts=(0, 1, 2, 3)):
                b, _ = made_in(b, g)
                if (c, g) == (0, 0):
                    pe.wait_ge(w_split, 2)
                    pe.wait_ge(w_split_v, qk_split_count())
                    pe.wait_ge(dve_read, rounds(b, DVE_READS, dve_reads(TILE_AT["T", KT - 1])))
                at = c * D + g * P
                out = free(b, "QK"[c], g) if parts[0] == 0 else bank[TILE_BANK[TILE_AT["QK"[c], g]]]
                last = exact_product(pe, out, [(wqkv_hi[:, k, at:at + P], wqkv_lo[:, k, at:at + P],
                                                fT_hi[:, k, :], fT_lo[:, k, :]) for k in parts],
                                     start=(parts[0] == 0), stop=(parts[-1] == KT - 1))
                if parts[-1] == KT - 1:
                    last.then_inc(tile_done, 1)

            transpose_tokens(-1)
            for c in range(2):
                project(0, c, 0)
            pe.wait_ge(tile_done, NT - TT)
            pe.sem_inc(tile_done, TT)
            with pe.Fori(0, B) as b:
                def values(t, parts=(0, 1, 2, 3)):
                    if t == 0:
                        pe.wait_ge(w_split_v, v_split_count())
                    out = free(b, "V", t) if parts[0] == 0 else bank[TILE_BANK[TILE_AT["V", t]]]
                    last = exact_product(pe, out, [(fT_hi[:, k, t * P:(t + 1) * P], fT_lo[:, k, t * P:(t + 1) * P],
                                                    wqkv_hi[:, k, 2 * D:3 * D], wqkv_lo[:, k, 2 * D:3 * D])
                                                   for k in parts], start=(parts[0] == 0), stop=(parts[-1] == KT - 1))
                    if parts[-1] == KT - 1:
                        last.then_inc(tile_done, 1)

                def scores(h):
                    c, s = h // 4, h // 4 % SLOTS
                    if h == 0:
                        pe.wait_ge(k_rows_in, 16)
                        pe.wait_ge(dve_read, rounds(b - 1, DVE_READS, dve_reads(TILE_AT["K", 0])))
                    if h % 4 == 0:
                        pe.wait_ge(stacked[s], stacked_count(b, c))
                    for k, tiles in enumerate(S_TILES):
                        pe.wait_ge(s_maxed, rounds(b, UNITS, 3 * h + k - 2))
                        at = 0
                        for t in tiles:
                            n = (t + 1) * P
                            pe.matmul(bank[k][:, at:at + n], q_st[0:K_MAX, s, h % 4, t * P:(t + 1) * P],
                                      k_st[0:K_MAX, s, h % 4, 0:n], start=True, stop=False)
                            last = pe.matmul(bank[k][:, at + n - P:at + n], identb[:, :], mask_qk[:, :],
                                             start=False, stop=True)
                            at += n
                        last.then_inc(s_done, 1)

                def transpose_maxima(c):
                    out = free(b, "M", c)
                    wait_apart(pe, apart["pe"], m_ready, rounds(b, NQ, c + 1))
                    pe.transpose(out[0:2 * 4 * TT, 0:P // 2].bitcast(BF16),
                                 mparts[:, :, :].rearrange("p a n -> p (a n)"), identb[:, :]).then_inc(tile_done, 1)

                def shifted_scores(h):
                    c, s = h // 4, h // 4 % SLOTS
                    if h == 0:
                        pe.wait_ge(act_read, rounds(b, ACT_READS, act_reads(TILE_AT["V", TT - 1])))
                        pe.wait_ge(dve_read, rounds(b, DVE_READS, dve_reads(TILE_AT["V", TT - 1])))
                    if h % 4 == 0:
                        pe.wait_ge(m_placed[c % 2], rounds(b, NQ // 2 * 32, (c // 2 + 1) * 32))
                    for k, tiles in enumerate(T_TILES):
                        pe.wait_ge(exp_done, rounds(b, UNITS, 3 * h + k - 2))
                        at = 0
                        for t in tiles:
                            n = S - t * P
                            pe.matmul(bank[3 + k][:, at:at + n], k_st[0:K_EXP, s, h % 4, t * P:(t + 1) * P],
                                      q_st[0:K_EXP, s, h % 4, t * P:S], start=True, stop=False)
                            last = pe.matmul(bank[3 + k][:, at:at + P], identb[:, :], mask_kq[:, :],
                                             start=False, stop=True)
                            at += n
                        last.then_inc(t_done, 1)

                def weigh_values(c, parts=(0, 1, 2, 3)):
                    if c == 0:
                        pe.wait_ge(dve_read, rounds(b, DVE_READS, dve_reads(TILE_AT["Q", 2])))
                    if parts[0] == 0:
                        pe.wait_ge(exp_done, rounds(b, UNITS, QU * (c + 1)))
                        pe.wait_ge(pv_copied, rounds(b, NQ, c))
                    for t in parts:
                        at = (0, 4 * P, 8 * P, 7 * P)[t]
                        n = S - t * P
                        for j in range(4):
                            last = pe.matmul(bank[6][32 * j:32 * j + 32, t * P:S], v_nat[:, t, 4 * c + j, :],
                                             pt[:, (4 * c + j) % PT_RING, at:at + n], start=(t == 0), stop=(t == TT - 1))
                    if parts[-1] == TT - 1:
                        last.then_inc(pv_done, 1)

                def project_between(h):
                    if h == 0:
                        pe.wait_ge(pv_copied, rounds(b, NQ, 0))
                    if h in BETWEEN:
                        c, g, half = BETWEEN[h]
                        project(b, c, g, half)

                def project_out():
                    for k in range(G):
                        if k == 0:
                            pe.wait_ge(w_split_v, v_split_count() + 1)
                        for t in range(TT):
                            half = t * P // HS
                            pe.wait_ge(attn_split, rounds(b, G * HALVES, k * HALVES + half + 1))
                            rows = slice(t * P, (t + 1) * P)
                            out = free(b, "P", t) if k == 0 else bank[TILE_BANK[TILE_AT["P", t]]]
                            last = exact_product(pe, out, [(aT_hi[:, k, rows], aT_lo[:, k, rows], wproj_hi[:, k, :],
                                                            wproj_lo[:, k, :])], start=(k == 0), stop=(k == G - 1))
                            if k == G - 1:
                                last.then_inc(tile_done, 1)

                values(0)
                values(1)
                for h in range(8):
                    scores(h)
                    half = ((0, 1), (2, 3))[h % 2]
                    if h < 4:
                        project(b, h // 2, 1, half)
                    else:
                        values(h // 2, half)
                    if h == 5:
                        transpose_maxima(0)
                for c in range(NQ):
                    for i in range(4):
                        shifted_scores(4 * c + i)
                        if c + 2 < NQ:
                            scores(4 * (c + 2) + i)
                        if i == 1 and c + 1 < NQ:
                            transpose_maxima(c + 1)
                        if i == 0 and c >= 1:
                            weigh_values(c - 1, (0,))
                        if i == 1 and c >= 1:
                            weigh_values(c - 1, (1, 2, 3))
                        if c <= 2:
                            project_between(4 * c + i)
                pe.wait_ge(s_maxed, rounds(b, UNITS, UNITS))
                pe.wait_ge(dve_read, rounds(b, DVE_READS, dve_reads(TILE_AT["M", NQ - 1])))
                transpose_tokens(b)
                weigh_values(NQ - 1)
                for c in range(2):
                    project(b + 1, c, 0)
                project_out()


def qk_split_count():
    return 1 + KT - 2


def v_split_count():
    return qk_split_count() + 1


def exact_product(pe, out, operands, start=True, stop=True):
    passes = [p for a_hi, a_lo, b_hi, b_lo in operands for p in ((a_hi, b_hi), (a_hi, b_lo), (a_lo, b_hi))]
    for i, (a, c) in enumerate(passes):
        last = pe.matmul(out[:, :], a, c, start=(start and i == 0), stop=(stop and i == len(passes) - 1))
    return last


def ffn(nc, tokens_dram, wgu_d, wd_d, out_d, bank, ident, minus_half, hT_hi, hT_lo, wgu_first, first_in, x1_stored):
    out_v = out_d.rearrange("b (t p) d -> b t p d", p=P)
    RAW = 3
    T_BANK = (6, 7, 4, 5)

    with ExitStack() as ctx:
        def sb(name, shape, dt=F32):
            return ctx.enter_context(nc.sbuf_tensor(name, shape, dt))

        def sem(name):
            return ctx.enter_context(nc.semaphore(name))

        wgu_hi = sb("wgu_hi", [P, FT, 2, KT, P], F32R)
        wgu_lo = sb("wgu_lo", [P, FT, 2, KT, P], F32R)
        wd_hi = sb("wd_hi", [P, FT, D], F32R)
        wd_lo = sb("wd_lo", [P, FT, D], F32R)
        wgu_raw = [wgu_first] + [sb(f"wgu_raw{i}", [P, 2, KT, P]) for i in range(1, RAW)]
        wd_raw = sb("wd_raw", [P, RAW, D])
        hn = sb("hn", [P, TT, D])
        x1 = sb("x1", [P, TT, D])
        stats = sb("stats2", [P, TT, 6])
        mv = sb("mv2", [P, TT, 2])
        rstd = sb("rstd2", [P, TT])
        silu = sb("silu", [P, 2, S])
        gu = sb("gu", [P, 2, S])
        gu_hi = sb("gu_hi", [P, 2, S], F32R)
        gu_lo = sb("gu_lo", [P, 2, S], F32R)

        wgu_in = [first_in] + [sem(f"wgu_in{i}") for i in range(1, RAW)]
        wd_in = [sem(f"wd_in{i}") for i in range(RAW)]
        w_hi_done = sem("w_hi_done2")
        w_lo_done = sem("w_lo_done2")
        hn_in = [sem(f"hn_in{t}") for t in range(TT)]
        x1_in = sem("x1_in")
        stats_made = sem("stats_made2")
        apart = {e: sem(f"apart2_{e}") for e in ("sp", "pool", "dve")}
        moments_ready = sem("moments_ready2")
        var_ready = sem("var_ready2")
        rstd_ready = sem("rstd_ready2")
        normed = sem("normed2")
        t_done = sem("t_done2")
        hi_done = sem("hi_done")
        lo_done = sem("lo_done")
        gate_done = sem("gate_done")
        up_done = sem("up_done")
        silu_done = sem("silu_done")
        gu_done = sem("gu_done")
        gu_hi_done = sem("gu_hi_done")
        gu_lo_done = sem("gu_lo_done")
        down_done = sem("down_done")
        sum_done = sem("sum_done")
        out_ready = sem("out_ready")
        out_stored = sem("out_stored")
        block = ctx.enter_context(nc.Block())

        @block.sync
        def _(sp):
            for s in hn_in:
                sp.sem_inc(s, 16)
            sp.sem_inc(out_stored, TT * 16)

            def load_weights(f):
                if f >= RAW:
                    sp.wait_ge(w_lo_done, 3 * (f - RAW + 1))
                if f > 0:
                    sp.dma_start(wgu_raw[f % RAW][:, :, :, :], wgu_d[f]).then_inc(wgu_in[f % RAW], 16)
                sp.dma_start(wd_raw[:, f % RAW, :], wd_d[f]).then_inc(wd_in[f % RAW], 16)

            def run_block(b):
                wait_apart(sp, apart["sp"], t_done, (b + 1) * KT)
                for t in range(TT):
                    sp.dma_start(hn[:, t, :], tokens_dram[(b + 1) % B + B, t]).then_inc(hn_in[t], 16)
                wait_apart(sp, apart["sp"], out_stored, rounds(b, TT * 16, 0))
                for t in range(TT):
                    sp.dma_start(x1[:, t, :], tokens_dram[b + B, t]).then_inc(x1_in, 16)
                if isinstance(b, int):
                    for f in range(RAW, FT):
                        load_weights(f)
                for t in range(TT):
                    wait_apart(sp, apart["sp"], out_ready, rounds(b, TT, t + 1))
                    sp.dma_start(out_v[b, t], x1[:, t, :]).then_inc(out_stored, 16)

            sp.wait_ge(x1_stored, rounds(B - 1, XR_INCS, XR_INCS))
            for f in range(RAW):
                load_weights(f)
            run_block(0)
            with sp.Fori(1, B) as b:
                run_block(b)
            sp.wait_ge(out_stored, rounds(B, TT * 16, 0))
            for t in range(TT):
                sp.wait_ge(hn_in[t], 16 * (B + 1))

        @block.gpsimd
        def _(pool):
            pool.sem_inc(var_ready, 1)
            pool.sem_inc(rstd_ready, 1)
            with pool.Fori(0, B) as b:
                inverse_deviation(pool, apart["pool"], mv, rstd, minus_half, moments_ready, var_ready, rstd_ready, b + 2)

        @block.scalar
        def _(act):
            for s, n in ((hi_done, KT), (silu_done, FT), (gu_hi_done, FT)):
                act.sem_inc(s, n)

            def weight_hi(f):
                act.wait_ge(wgu_in[f % RAW], 16 * (f // RAW + 1))
                for c in range(2):
                    act.copy(wgu_hi[:, f, c, :, :], wgu_raw[f % RAW][:, c, :, :]).then_inc(w_hi_done, 1)
                act.wait_ge(wd_in[f % RAW], 16 * (f // RAW + 1))
                act.copy(wd_hi[:, f, :], wd_raw[:, f % RAW, :]).then_inc(w_hi_done, 1)

            def transposed_hi(n):
                for k in range(KT):
                    act.wait_ge(t_done, n * KT + k + 1)
                    act.copy(hT_hi[:, k, :], bank[T_BANK[k]][:, :]).then_inc(hi_done, 1)

            def run_block(b):
                def gate(f):
                    act.wait_ge(gate_done, rounds(b, FT, f + 1))
                    act.wait_ge(gu_done, rounds(b, FT, f - 1))
                    act.activation(silu[:, f % 2, :], bank[4 + 2 * (f % 2)][:, :], ACT.Silu).then_inc(silu_done, 1)

                def high(f):
                    act.wait_ge(gu_done, rounds(b, FT, f + 1))
                    act.wait_ge(down_done, rounds(b, FT, f - 1))
                    act.copy(gu_hi[:, f % 2, :], gu[:, f % 2, :]).then_inc(gu_hi_done, 1)

                for f in range(FT):
                    gate(f)
                    high(f)
                    if isinstance(b, int) and f + 2 < FT:
                        weight_hi(f + 2)
                transposed_hi(b + 1)

            weight_hi(0)
            weight_hi(1)
            run_block(0)
            with act.Fori(1, B) as b:
                run_block(b)

        @block.vector
        def _(dve):
            for s, n in ((stats_made, TT), (moments_ready, 1), (normed, 1), (lo_done, KT), (gu_done, FT), (gu_lo_done, FT),
                         (out_ready, TT)):
                dve.sem_inc(s, n)

            def weight_lo(f):
                for c in range(2):
                    dve.wait_ge(w_hi_done, 3 * f + c + 1)
                    dve.tensor_tensor(wgu_lo[:, f, c, :, :], wgu_raw[f % RAW][:, c, :, :],
                                      wgu_hi[:, f, c, :, :].bitcast(F32), ALU.subtract).then_inc(w_lo_done, 1)
                dve.wait_ge(w_hi_done, 3 * f + 3)
                dve.tensor_tensor(wd_lo[:, f, :], wd_raw[:, f % RAW, :], wd_hi[:, f, :].bitcast(F32),
                                  ALU.subtract).then_inc(w_lo_done, 1)

            def token_statistics(n, t):
                dve.wait_ge(hn_in[t], (n + 1) * 16)
                statistics(dve, hn, stats, t).then_inc(stats_made, 1)

            def token_moments(n):
                wait_apart(dve, apart["dve"], stats_made, (n + 1) * TT)
                moments(dve, stats, mv, moments_ready)

            def normalised(n):
                normalise(dve, hn, hn, mv, rstd, moments_ready, rstd_ready, n + 1).then_inc(normed, 1)

            def transposed_lo(n):
                for k in range(KT):
                    dve.wait_ge(hi_done, n * KT + k + 1)
                    dve.tensor_tensor(hT_lo[:, k, :], bank[T_BANK[k]][:, :], hT_hi[:, k, :].bitcast(F32),
                                      ALU.subtract).then_inc(lo_done, 1)

            def run_block(b):
                for f in range(FT):
                    dve.wait_ge(silu_done, rounds(b, FT, f + 1))
                    dve.wait_ge(up_done, rounds(b, FT, f + 1))
                    dve.wait_ge(gu_hi_done, rounds(b, FT, f - 1))
                    dve.tensor_tensor(gu[:, f % 2, :], bank[5 + 2 * (f % 2)][:, :], silu[:, f % 2, :],
                                      ALU.mult).then_inc(gu_done, 1)
                    dve.wait_ge(gu_hi_done, rounds(b, FT, f + 1))
                    dve.tensor_tensor(gu_lo[:, f % 2, :], gu[:, f % 2, :], gu_hi[:, f % 2, :].bitcast(F32),
                                      ALU.subtract).then_inc(gu_lo_done, 1)
                    if isinstance(b, int) and f + 2 < FT:
                        weight_lo(f + 2)
                    if 3 <= f < 3 + TT:
                        token_statistics(b + 1, f - 3)
                    if f == 3 + TT:
                        token_moments(b + 1)
                    if f == 4 + TT:
                        normalised(b + 1)
                transposed_lo(b + 1)
                dve.wait_ge(x1_in, (b + 1) * 16 * TT)
                for t in range(TT):
                    dve.wait_ge(sum_done, b * TT + t + 1)
                    dve.tensor_tensor(x1[:, t, :], bank[t][:, :], x1[:, t, :], ALU.add).then_inc(out_ready, 1)

            weight_lo(0)
            weight_lo(1)
            run_block(0)
            with dve.Fori(1, B) as b:
                run_block(b)

        @block.tensor
        def _(pe):
            for s, n in ((t_done, KT), (gate_done, FT), (up_done, FT), (down_done, FT)):
                pe.sem_inc(s, n)

            def transpose_tokens(b):
                pe.wait_ge(normed, b + 2)
                for k in range(KT):
                    if k in (0, 2):
                        pe.wait_ge(gu_done, rounds(b, FT, FT - 1 + k // 2))
                    for t in range(TT):
                        last = pe.transpose(bank[T_BANK[k]][:, t * P:(t + 1) * P], hn[:, t, k * P:(k + 1) * P], ident[:, :])
                    last.then_inc(t_done, 1)

            def run_block(b):
                def gate_up(f):
                    if f == 0:
                        pe.wait_ge(lo_done, (b + 1) * KT)
                    for c, done in enumerate((gate_done, up_done)):
                        if isinstance(b, int):
                            pe.wait_ge(w_lo_done, 3 * f + c + 1)
                        pe.wait_ge(gu_done, rounds(b, FT, f - 1))
                        exact_product(pe, bank[4 + 2 * (f % 2) + c],
                                      [(wgu_hi[:, f, c, k, :], wgu_lo[:, f, c, k, :], hT_hi[:, k, :], hT_lo[:, k, :])
                                       for k in range(KT)]).then_inc(done, 1)

                def down(f):
                    if f == 0:
                        pe.wait_ge(out_ready, rounds(b, TT, 0))
                    if isinstance(b, int):
                        pe.wait_ge(w_lo_done, 3 * f + 3)
                    pe.wait_ge(gu_lo_done, rounds(b, FT, f + 1))
                    for t in range(TT):
                        cols = slice(t * P, (t + 1) * P)
                        for i, (a, w) in enumerate(((gu_hi, wd_hi), (gu_hi, wd_lo), (gu_lo, wd_hi))):
                            last = pe.matmul(bank[t][:, :], a[:, f % 2, cols], w[:, f, :],
                                             start=(f == 0 and i == 0), stop=(f == FT - 1 and i == 2))
                        if f == FT - 1:
                            last.then_inc(sum_done, 1)
                    if f < FT - 1:
                        last.then_inc(down_done, 1)
                    else:
                        pe.wait_ge(sum_done, b * TT + TT)
                        pe.sem_inc(down_done, 1)

                gate_up(0)
                for f in range(1, FT):
                    gate_up(f)
                    down(f - 1)
                transpose_tokens(b)
                down(FT - 1)

            run_block(0)
            with pe.Fori(1, B) as b:
                run_block(b)


def kernel(**inputs):
    from concourse import bacc
    from concourse.bass_utils import run_bass_kernel_spmd

    def given(name):
        return np.ascontiguousarray(inputs["L0_" + name])

    def padded(w):
        return np.concatenate([w, np.zeros((FT * P - F, D), w.dtype)])

    both = np.stack([padded(given("ffn_w_gate")), padded(given("ffn_w_up"))])
    wgu = np.ascontiguousarray(both.reshape(2, FT, P, KT, P).transpose(1, 4, 0, 3, 2))
    wd = np.ascontiguousarray(padded(given("ffn_w_down").T).reshape(FT, P, D))
    q_rows, k_rows = extra_rows()

    def stacked_order(w):
        qk = w[..., :2 * D].reshape(*w.shape[:-1], 2 * G, HG, HD).swapaxes(-1, -2).reshape(*w.shape[:-1], 2 * D)
        return np.ascontiguousarray(np.concatenate([qk, w[..., 2 * D:]], -1))

    arrays = {
        "x": given("attn_hidden_states"), "w_qkv": stacked_order(given("attn_w_attn")),
        "b_qkv": stacked_order(given("attn_b_attn")),
        "w_proj": given("attn_w_proj"), "b_proj": given("attn_b_proj"), "w_gate_up": wgu, "w_down": wd,
        "q_rows": q_rows, "k_rows": k_rows,
    }
    nc = bacc.Bacc("TRN2", target_bir_lowering=False, num_devices=1)
    args = [nc.dram_tensor(n, a.shape, mybir.dt.from_np(a.dtype), kind="ExternalInput").ap() for n, a in arrays.items()]
    out = nc.dram_tensor("out", (B, S, D), F32, kind="ExternalOutput").ap()
    kernel_body(nc, *args, out)
    return run_bass_kernel_spmd(nc, [arrays], core_ids=[0]).results[0]["out"]
```
